# Optimizing a Trainium2 kernel written in Bass

```python
import numpy as np
import jax
import jax.numpy as jnp

def _softmax(x, axis=-1):
    return jax.nn.softmax(x, axis=axis)

def _gelu(x):
    return jax.nn.gelu(x, approximate=True)

def _silu(x):
    return jax.nn.silu(x)

def _sigmoid(x):
    return jax.nn.sigmoid(x)

def _layernorm(x, axis=-1, eps=1e-05):
    m = jnp.mean(x, axis=axis, keepdims=True)
    v = jnp.var(x, axis=axis, keepdims=True)
    return (x - m) / jnp.sqrt(v + eps)

def _scatter_add(tgt, idx, src, axis=0):
    return tgt.at[idx].add(src)

def _segment_sum(src, seg, n):
    return jax.ops.segment_sum(src, seg, n)
kernel_name = 'mk_adj_preln_d4_adj_r2_b240e2'

def setup_inputs(seed: int=0):
    np.random.seed(seed)
    _w = jnp.asarray

    def _rec_inputs():
        import jax
        import jax.numpy as jnp
        _gk = jax.random.key(seed)
        x = 0.0002279 + 0.9999 * jax.random.normal(jax.random.fold_in(_gk, 1), (8192, 128), jnp.float32)
        _a = jax.random.bernoulli(jax.random.fold_in(_gk, 2), 0.000488281, (8192, 8192))
        adj = _a.astype(jnp.int32)
        return (x, adj)
    x, adj = _rec_inputs()

    def _L0_gnn_setup():
        import jax, jax.numpy as jnp
        import numpy as np
        N = 4096
        IN_F = 128
        OUT_F = 128
        ALPHA = 0.2
        NEG_FILL = -9000000000000000.0
        key = jax.random.key(seed)
        k_adj, k_h, k_w, k_a = jax.random.split(key, 4)
        adj = jax.random.randint(k_adj, (N, N), 0, 2, dtype=jnp.int32)
        h = jax.random.normal(k_h, (N, IN_F), dtype=jnp.float32)
        W = jax.random.normal(k_w, (IN_F, OUT_F), dtype=jnp.float32) * (2.0 / (IN_F + OUT_F)) ** 0.5
        a = jax.random.normal(k_a, (2 * OUT_F, 1), dtype=jnp.float32) * (2.0 / (2 * OUT_F + 1)) ** 0.5
        return {'adj': adj, 'h': h, 'W': W, 'a': a}
    _L0_gnn_all = _L0_gnn_setup()
    _L0_gnn_in = {k: v for k, v in _L0_gnn_all.items() if k in ('W', 'a')}
    del _L0_gnn_all

    def _L1_gnn_setup():
        import jax, jax.numpy as jnp
        import numpy as np
        N = 4096
        IN = 128
        OUT = 128
        THR = 0.0001
        ALPHA = 0.2
        NEG = -1000000000.0
        key = jax.random.key(seed)
        k1, k2, k3, k4 = jax.random.split(key, 4)
        inp = jax.random.normal(k1, (N, IN), jnp.float32)
        W = jax.random.normal(k2, (IN, OUT), jnp.float32) * (1.414 * np.sqrt(2.0 / (IN + OUT)))
        a = jax.random.normal(k3, (2 * OUT, 1), jnp.float32) * (1.414 * np.sqrt(2.0 / (2 * OUT + 1)))
        adj = jax.random.randint(k4, (N, N), 0, 2, jnp.int32)
        return {'input': inp, 'W': W, 'a': a, 'adj': adj, 'M': N}
    _L1_gnn_all = _L1_gnn_setup()
    _L1_gnn_in = {k: v for k, v in _L1_gnn_all.items() if k in ('W', 'a')}
    del _L1_gnn_all

    def _L2_gnn_setup():
        import jax, jax.numpy as jnp
        import numpy as np
        NEG_INF = -9000000000000000.0
        ALPHA = 0.2
        key = jax.random.key(seed)
        k1, k2, k3, k4 = jax.random.split(key, 4)
        N, F_IN, H, D = (4096, 128, 4, 32)
        h = jax.random.normal(k1, (N, F_IN), dtype=jnp.float32)
        adj = jax.random.randint(k2, (N, N), 0, 2, dtype=jnp.int32)
        W = jax.random.normal(k3, (F_IN, H * D), dtype=jnp.float32) * (1.0 / np.sqrt(F_IN))
        a = jax.random.normal(k4, (1, H, 2 * D), dtype=jnp.float32)
        return {'h': h, 'adj': adj, 'W': W, 'a': a}
    _L2_gnn_all = _L2_gnn_setup()
    _L2_gnn_in = {k: v for k, v in _L2_gnn_all.items() if k in ('W', 'a')}
    del _L2_gnn_all

    def _L3_gnn_setup():
        import jax, jax.numpy as jnp
        import numpy as np
        N = 4096
        D_IN = 128
        D_OUT = 128
        ALPHA = 0.2
        NEG = -9000000000000000.0
        key = jax.random.key(seed)
        k1, k2, k3, k4 = jax.random.split(key, 4)
        input = jax.random.normal(k1, (N, D_IN), dtype=jnp.float32)
        adj = jax.random.randint(k2, (N, N), 0, 2, dtype=jnp.int32)
        lim_w = 1.414 * np.sqrt(6.0 / (D_IN + D_OUT))
        W = jax.random.uniform(k3, (D_IN, D_OUT), jnp.float32, -lim_w, lim_w)
        lim_a = 1.414 * np.sqrt(6.0 / (2 * D_OUT + 1))
        a = jax.random.uniform(k4, (2 * D_OUT, 1), jnp.float32, -lim_a, lim_a)
        return {'input': input, 'adj': adj, 'W': W, 'a': a}
    _L3_gnn_all = _L3_gnn_setup()
    _L3_gnn_in = {k: v for k, v in _L3_gnn_all.items() if k in ('W', 'a')}
    del _L3_gnn_all
    return {'x': x, 'adj': adj, 'L0_gnn_W': _L0_gnn_in['W'], 'L0_gnn_a': _L0_gnn_in['a'], 'L1_gnn_W': _L1_gnn_in['W'], 'L1_gnn_a': _L1_gnn_in['a'], 'L2_gnn_W': _L2_gnn_in['W'], 'L2_gnn_a': _L2_gnn_in['a'], 'L3_gnn_W': _L3_gnn_in['W'], 'L3_gnn_a': _L3_gnn_in['a']}

def reference(x, adj, L0_gnn_W, L0_gnn_a, L1_gnn_W, L1_gnn_a, L2_gnn_W, L2_gnn_a, L3_gnn_W, L3_gnn_a):
    import jax
    import jax.numpy as jnp

    def _L0_gnn_ref(adj, h, W, a):
        import jax, jax.numpy as jnp
        import numpy as np
        N = 4096
        IN_F = 128
        OUT_F = 128
        ALPHA = 0.2
        NEG_FILL = -9000000000000000.0
        Wh = h @ W
        Wh1 = Wh @ a[:OUT_F, :]
        Wh2 = Wh @ a[OUT_F:, :]
        e = jax.nn.leaky_relu(Wh1 + Wh2.T, ALPHA)
        attention = jnp.where(adj > 0, e, jnp.float32(NEG_FILL))
        attention = jax.nn.softmax(attention, axis=1)
        h_prime = attention @ Wh
        return jax.nn.elu(h_prime)

    def _L1_gnn_ref(input, W, a, adj, M):
        import jax, jax.numpy as jnp
        import numpy as np
        N = 4096
        IN = 128
        OUT = 128
        THR = 0.0001
        ALPHA = 0.2
        NEG = -1000000000.0
        h = input @ W
        a_src = a[:OUT, 0]
        a_dst = a[OUT:, 0]
        e = jax.nn.leaky_relu((h[:M] @ a_src)[:, None] + (h @ a_dst)[None, :], negative_slope=ALPHA)
        valid = (adj[:M] > 0) & (h.sum(axis=1) != 0)[None, :]
        att = jax.nn.softmax(jnp.where(valid, e, NEG), axis=1)
        att = jnp.where(valid, att, 0.0)
        L = valid.sum(axis=1).astype(h.dtype)
        top = att.max(axis=1)
        attention = jnp.where(att >= THR, att, 0.0) * L[:, None]
        attention = jnp.where((top > THR)[:, None], attention, 0.0)
        h_prime = attention @ h
        return jax.nn.elu(h[:M] + h_prime)

    def _L2_gnn_ref(h, adj, W, a):
        import jax, jax.numpy as jnp
        import numpy as np
        NEG_INF = -9000000000000000.0
        ALPHA = 0.2
        N = h.shape[0]
        H = a.shape[1]
        D = a.shape[2] // 2
        Wh = (h @ W).reshape(N, H, D)
        a_src = a[0, :, :D]
        a_dst = a[0, :, D:]
        s_src = jnp.einsum('nhd,hd->nh', Wh, a_src)
        s_dst = jnp.einsum('nhd,hd->nh', Wh, a_dst)
        e = s_src[:, None, :] + s_dst[None, :, :]
        e = jnp.where(e >= 0, e, ALPHA * e)
        e = jnp.where(adj[:, :, None] > 0, e, NEG_INF)
        attention = jax.nn.softmax(e, axis=1)
        h_prime = jnp.einsum('ijh,jhd->ihd', attention, Wh)
        return jax.nn.elu(h_prime.reshape(N, H * D))

    def _L3_gnn_ref(input, adj, W, a):
        import jax, jax.numpy as jnp
        import numpy as np
        N = 4096
        D_IN = 128
        D_OUT = 128
        ALPHA = 0.2
        NEG = -9000000000000000.0
        h = input @ W
        a1 = a[:D_OUT, 0]
        a2 = a[D_OUT:, 0]
        e = (h @ a1)[:, None] + (h @ a2)[None, :]
        e = jnp.where(e > 0, e, ALPHA * e)
        e = jnp.where(adj > 0, e, NEG)
        attention = jax.nn.softmax(e, axis=1)
        h_prime = attention @ h
        return jax.nn.elu(h_prime)
    h = jnp.maximum(_layernorm(x, axis=-1), 0.0)
    x = x + _L0_gnn_ref(adj, h, L0_gnn_W, L0_gnn_a)
    h = jnp.maximum(_layernorm(x, axis=-1), 0.0)
    x = x + _L1_gnn_ref(h, L1_gnn_W, L1_gnn_a, adj, 8192)
    h = jnp.maximum(_layernorm(x, axis=-1), 0.0)
    x = x + _L2_gnn_ref(h, adj, L2_gnn_W, L2_gnn_a)
    h = jnp.maximum(_layernorm(x, axis=-1), 0.0)
    x = x + _L3_gnn_ref(h, adj, L3_gnn_W, L3_gnn_a)
    return x

_drawn_inputs = setup_inputs


def setup_inputs(seed=0):
    import zlib

    import numpy as np

    out = dict(_drawn_inputs(seed))
    spreads = {}
    factors = {}
    for name, (base, spread) in spreads.items():
        noise = np.random.default_rng([zlib.crc32(name.encode()), seed]).standard_normal(out[name].shape)
        drawn = base * np.exp(spread * noise) if base else spread * noise
        out[name] = jnp.asarray(drawn.astype(out[name].dtype))
    for name, factor in factors.items():
        out[name] = (out[name] * factor).astype(out[name].dtype)
    return out
```

```python
from contextlib import ExitStack

import concourse.bass as bass
from concourse import mybir

ALU = mybir.AluOpType
ACT = mybir.ActivationFunctionType
AX = mybir.AxisListType
F32 = mybir.dt.float32
BF16 = mybir.dt.bfloat16
U8 = mybir.dt.uint8
U16 = mybir.dt.uint16
U32 = mybir.dt.uint32
I32 = mybir.dt.int32

P = 128
EPS = 1e-5
ALPHA = 0.2
THR = 1e-4
BIG = 2.0 ** 100
FLOOR = -2.0 ** 90
SLOTS = 16
HEADS = [1, 1, 4, 1]

FIRST_QUAD = [16, 9, 8, 8]
QUAD_SLOTS = [7, 6, 6, 5, 5, 5, 4, 4, 4, 3, 3, 3, 2, 2, 1]

R_S, R_NL, R_ID, RW = 128, 132, 148, 152
T_T, T_AUX, T_S, TW = 128, 129, 132, 136


def slots_of(quad, j):
    return FIRST_QUAD[j] if quad == 0 else QUAD_SLOTS[quad - 1]


def runs(quads):
    out = []
    for q in range(quads):
        k = None if q == 0 else QUAD_SLOTS[q - 1]
        if out and q != quads - 1 and out[-1][2] == k:
            out[-1][1] += 1
        else:
            out.append([q, 1, k])
    return out


def gat_kernel(nc, x, adj, W0, a0, W1, a1, W2, a2, W3, a3, out):
    N, F = x.shape
    T = N // P
    QUADS = T // 4
    HALF = N // 2
    HP = HALF // 2
    SEG = 512
    SEGS = HP // SEG
    CAND = 2 * SEGS * 8
    NC = SLOTS + 1
    ODD0 = N + 1
    RUNS = runs(QUADS)
    Ws, As = [W0, W1, W2, W3], [a0, a1, a2, a3]

    rec_d = nc.dram_tensor("records_sorted", (N, RW), F32, kind="Internal").ap()
    tab_d = [nc.dram_tensor(f"table_{l}", (N, TW), F32, kind="Internal").ap() for l in range(4)]

    with ExitStack() as ctx:
        def sb(name, shape, dt):
            return ctx.enter_context(nc.sbuf_tensor(name, shape, dt))

        def sem(name):
            return ctx.enter_context(nc.semaphore(name))

        REC = sb("REC", [P, T, RW], F32)
        TBL = sb("TBL", [P, T, TW], F32)
        WA = sb("WA", [P, 4, TW], F32)
        WT = sb("WT", [P, P], F32)
        AV = sb("AV", [P, 4, 8], F32)
        IDN = sb("IDN", [P, P], F32)
        ONE = sb("ONE", [P, P], F32)
        ONEN = sb("ONEN", [P, P], F32)
        MEAN = sb("MEAN", [P, F], F32)
        C100 = sb("C100", [P, 1], F32)
        ST = sb("ST", [P, 2, 6], F32)
        MV = sb("MV", [P, 2, 2], F32)
        VAR = sb("VAR", [P, T], F32)
        RSTD = sb("RSTD", [P, T], F32)
        NEWT = sb("NEWT", [P, T], F32)
        SEED = sb("SEED", [P, T], I32)
        HN = sb("HN", [P, 2, F], F32)
        HT = sb("HT", [P, 2, F], F32)
        NLU = sb("NLU", [P, T, SLOTS], U32)
        DEGH = sb("DEGH", [P, 2 * T], F32)
        COUNT = sb("COUNT", [P, T], F32)
        RANKF = sb("RANKF", [P, T], F32)
        RANKU = sb("RANKU", [P, T], U32)
        FLAG = sb("FLAG", [P, 4], F32)
        FLAGI = sb("FLAGI", [P, 1], I32)

        AREA = sb("AREA", [P, 4, HALF], I32)
        AREB = sb("AREB", [P, 8192], F32)
        area = AREA[:].rearrange("p a b -> p (a b)")

        mask = AREB[:, 0:2048].bitcast(U8).rearrange("p (b n) -> p b n", b=2)
        pair_code = AREB[:, 2048:4096].bitcast(U16)
        code = AREB[:, 4096:8192].rearrange("p (b n) -> p b n", b=2)
        CODES = sb("CODES", [P, T, SLOTS], F32)
        CND = sb("CND", [P, CAND], F32)
        CND2 = sb("CND2", [P, CAND], F32)
        TOP = sb("TOP", [P, SLOTS], F32)

        def part(base, shape, dt=F32):
            n = 1
            for s in shape:
                n *= s
            v = area[:, base:base + (n if dt in (F32, U32, I32) else n // 2)].bitcast(dt)
            names = "abcd"[:len(shape)]
            if len(shape) == 1:
                return v
            return v.rearrange(f"p ({' '.join(names)}) -> p {' '.join(names)}",
                               **dict(zip(names, shape)))

        D_I = part(0, [T * SLOTS], I32)
        D_ODD = part(1024, [T * SLOTS])
        D_B = part(2048, [T * SLOTS])
        D_Q = part(3072, [T * SLOTS])
        D_W = part(4096, [T * SLOTS])
        L32 = part(5120, [T, 2 * SLOTS])
        S32 = part(7168, [4, 2 * SLOTS])
        S32B = part(7296, [4, 2 * SLOTS])
        S16 = part(7424, [4, SLOTS])
        CLS = part(7680, [NC, T])
        OH = part(8832, [NC, T])
        OHB = part(9984, [NC, T], BF16)
        TOT = part(10624, [NC, T])
        SC = [part(11776, [NC, T]), part(12928, [NC, T])]
        CT = [part(14080, [NC + 1]), part(14112, [NC + 1])]
        UPPER = part(14144, [P], BF16)
        ONEB = part(14208, [P], BF16)
        TMP = part(14336, [T, 2 * SLOTS])
        MIS = part(4096, [T])

        G = part(0, [4, SLOTS, TW])
        PR = part(14080, [SLOTS, F])
        IX = part(8704, [4, SLOTS], U32)
        VB = part(10560, [T, SLOTS])
        D0 = part(11584, [T])
        SCO = part(11648, [SLOTS + 1, 4])
        PRB = part(11728, [SLOTS, 4])
        MX = part(11792, [4])
        Z = part(11796, [4])
        RZ = part(11800, [4])
        AUX1 = part(11804, [SLOTS])
        AUX2 = part(11820, [SLOTS])
        LCNT = part(11836, [4])
        TOPA = part(11840, [4])
        CO = part(11844, [4])
        ACC = part(11904, [F])
        HH = part(12032, [F])
        EN = part(12160, [F])
        EX = part(12288, [F])
        OX = part(12416, [4, F])
        IDU = part(12928, [4], U32)
        PADS = part(12992, [T, SLOTS])

        X_ADJ = part(0, [N], I32)
        X_BIAS = part(0, [N])
        X_E = part(N, [N])
        X_T = AREB[:, 0:N]
        X_TC = CODES[:].rearrange("p t s -> p (t s)")[:, 0:T]
        X_TG = CODES[:].rearrange("p t s -> p (t s)")[:, T:2 * T]
        X_DIAG = sb("X_DIAG", [P, 2, P], F32)
        X_PT = sb("X_PT", [P, 2, 4 * P], F32)
        X_ST = sb("X_ST", [P, 2, 4 * P], F32)
        X_M = sb("X_M", [P, 8], F32)
        X_H = sb("X_H", [P, F], F32)
        X_E1 = sb("X_E1", [P, F], F32)
        ZERO = sb("ZERO", [P, P], F32)

        def ps(name):
            return ctx.enter_context(nc.psum_tensor(name, [P, 512], F32))

        psT = [ps("psT0"), ps("psT1")]
        psW = [ps("psW0"), ps("psW1")]
        psM = [ps("psM0"), ps("psM1")]
        psX = [ps("psX0"), ps("psX1")]

        x_loaded = sem("x_loaded")
        w_loaded = sem("w_loaded")
        av_zeroed = sem("av_zeroed")
        consts = sem("consts")
        iotas = sem("iotas")
        wt_made = sem("wt_made")
        wt_copied = sem("wt_copied")
        wa_made = sem("wa_made")
        wa_copied = sem("wa_copied")
        adj_loaded = [sem(f"adj_loaded{b}") for b in range(4)]
        mask_made = sem("mask_made")
        mask_read = sem("mask_read")
        hn_made = sem("hn_made")
        ht_psum = sem("ht_psum")
        ht_made = sem("ht_made")
        wh_made = sem("wh_made")
        raw_kept = sem("raw_kept")
        rstd_made = sem("rstd_made")
        tb_made = sem("tb_made")
        mean_made = sem("mean_made")
        extracted = sem("extracted")
        onehot_made = sem("onehot_made")
        prefix_made = sem("prefix_made")
        miss_made = sem("miss_made")
        flag_summed = sem("flag_summed")
        flag_ready = sem("flag_ready")
        rank_ready = sem("rank_ready")
        table_stored = sem("table_stored")
        rec_scattered = sem("rec_scattered")
        rec_loaded = sem("rec_loaded")
        ix_staged = sem("ix_staged")
        gathered = [sem(f"gathered{b}") for b in range(4)]
        sc_made = sem("sc_made")
        exp_made = sem("exp_made")
        en_made = sem("en_made")
        ex_made = sem("ex_made")
        ox_made = sem("ox_made")
        ox_stored = [sem(f"ox_stored{b}") for b in range(4)]
        upper_made = sem("upper_made")
        x_adj = sem("dense_adj_loaded")
        x_adj_free = sem("dense_adj_free")
        x_diag = sem("dense_diag_made")
        x_tb = sem("dense_t_spread")
        x_tbc = sem("dense_t_copied")
        x_sc = sem("dense_scores_made")
        x_exp = sem("dense_exp_made")
        x_pr = sem("dense_weights_ready")
        x_stg = sem("dense_block_staged")
        x_tr = sem("dense_transposed")
        x_trc = sem("dense_transposed_copied")
        x_acc = sem("dense_summed")
        x_en = sem("dense_en_made")
        x_ex = sem("dense_ex_made")
        x_out = sem("dense_out_made")
        x_stored = sem("dense_out_stored")

        block = ctx.enter_context(nc.Block())

        def gathers_before(b, quad, run):
            q0, n, k = run
            before = sum(slots_of(q, b) for q in range(q0))
            if n == 1:
                return 16 * before
            return 16 * before + (quad - q0) * (16 * k)

        GPL = [16 * sum(slots_of(q, b) for q in range(QUADS)) for b in range(4)]

        INST = [(l, h) for l in range(4) for h in range(HEADS[l])]

        def over(eng, run):
            q0, n, _ = run
            if n == 1:
                yield q0
            else:
                with eng.Fori(q0, q0 + n) as q:
                    yield q

        def deviations(dve, v, t, n):
            at = bass.ds(t, n)
            y, x, u = RSTD[:, at], VAR[:, at], NEWT[:, 0:n]
            dve.drain()
            v.tensor_scalar(SEED[:, 0:n], x.bitcast(I32), 1, None, ALU.arith_shift_right)
            dve.drain()
            v.tensor_scalar(y.bitcast(I32), SEED[:, 0:n], -1.0, float(0x5F3759DF), ALU.mult, ALU.add)
            dve.drain()
            for step in range(4):
                v.tensor_tensor(u, y, y, ALU.mult)
                dve.drain()
                v.scalar_tensor_tensor(u, u, -0.5, x, ALU.mult, ALU.mult)
                dve.drain()
                last = v.scalar_tensor_tensor(y, u, 1.5, y, ALU.add, ALU.mult)
                if step == 3:
                    last.then_inc(rstd_made, 1)
                else:
                    dve.drain()

        def layer_mean(dve, v, l):
            if l > 0:
                dve.wait_ge(mean_made, T * (l + 1))
                dve.wait_ge(tb_made, T * (l + 1))
                v.tensor_copy(MEAN[:], psM[l % 2][:, 0:F])
                dve.drain()

        def fast(dve, v, norm):
            dve.wait_ge(rec_loaded, 16)
            NL = REC[:, :, R_NL:R_NL + SLOTS]
            v.memset(G, 0.0)
            v.memset(SCO[:, SLOTS, :], FLOOR)
            v.tensor_scalar(VB, NL, 0.0, -BIG, ALU.is_equal, ALU.mult)
            v.tensor_scalar(D0, REC[:, :, R_NL], 0.0, None, ALU.is_equal)
            v.tensor_scalar(PADS, NL, 0.0, 2.0 * N, ALU.is_equal, ALU.mult)
            dve.drain()
            v.scalar_tensor_tensor(NLU[:], NL, -1.0, PADS, ALU.add, ALU.add)
            dve.drain()
            v.tensor_copy(IX, NLU[:, 0:4, :]).then_inc(ix_staged, 4)
            for l in range(4):
                layer_mean(dve, v, l)
                for run in RUNS:
                    for q in over(dve, run):
                        for b in range(4):
                            fast_tile(dve, v, norm, l, run, q, b)

        def fast_tile(dve, v, norm, l, run, q, b):
            H = HEADS[l]
            k = slots_of(run[0], b)
            t = 4 * q + b
            no = l * T + t
            lo = SLOTS - k
            per_head = lambda ap: ap.unsqueeze(1).to_broadcast([P, k, H])
            sco = SCO[:, lo:SLOTS, 0:H]
            rows = G[:, b, 0:k, 0:F]

            dve.wait_ge(gathered[b], l * GPL[b] + gathers_before(b, q, run) + 16 * k)
            v.tensor_tensor(sco, G[:, b, 0:k, T_T:T_T + H], per_head(REC[:, t, R_S:R_S + H] if l == 0 else TBL[:, t, T_S:T_S + H]), ALU.add)
            if l == 1:
                v.tensor_scalar(AUX1[:, 0:k], G[:, b, 0:k, T_AUX], 0.0, 1.0, ALU.not_equal, ALU.subtract)
            dve.drain()
            v.scalar_tensor_tensor(sco, sco, ALPHA, sco, ALU.mult, ALU.max)
            if l == 1:
                v.scalar_tensor_tensor(AUX1[:, 0:k], AUX1[:, 0:k], BIG, VB[:, t, 0:k], ALU.mult, ALU.add)
            dve.drain()
            if l == 1:
                v.tensor_tensor(SCO[:, lo:SLOTS, 0], SCO[:, lo:SLOTS, 0], AUX1[:, 0:k], ALU.add)
                v.tensor_scalar(AUX2[:, 0:k], AUX1[:, 0:k], 0.0, None, ALU.is_equal)
            else:
                v.tensor_tensor(sco, sco, VB[:, t, 0:k].unsqueeze(2).to_broadcast([P, k, H]), ALU.add)
            dve.drain()
            v.tensor_reduce(MX[:, 0:H], SCO[:, lo:SLOTS + 1, 0:H].rearrange("p s h -> p h s"), AX.X, ALU.max)
            if l == 1:
                v.tensor_reduce(LCNT[:, 0:1], AUX2[:, 0:k], AX.X, ALU.add)
            dve.drain()
            v.tensor_tensor(sco, sco, per_head(MX[:, 0:H]), ALU.subtract).then_inc(sc_made, 1)

            dve.wait_ge(exp_made, no + 1)
            v.tensor_reduce(Z[:, 0:H], PRB[:, 0:k, 0:H].rearrange("p s h -> p h s"), AX.X, ALU.add)
            dve.drain()
            v.tensor_scalar(Z[:, 0:H], Z[:, 0:H], 1e-30, None, ALU.max)
            dve.drain()
            v.reciprocal(RZ[:, 0:H], Z[:, 0:H])
            if l == 1:
                dve.drain()
                v.tensor_scalar(AUX1[:, 0:k], PRB[:, 0:k, 0], RZ[:, 0:1], None, ALU.mult)
                dve.drain()
                v.tensor_reduce(TOPA[:, 0:1], AUX1[:, 0:k], AX.X, ALU.max)
                v.scalar_tensor_tensor(PRB[:, 0:k, 0], AUX1[:, 0:k], THR, AUX1[:, 0:k], ALU.is_ge, ALU.mult)
                dve.drain()
                v.scalar_tensor_tensor(RZ[:, 0:1], TOPA[:, 0:1], THR, LCNT[:, 0:1], ALU.is_gt, ALU.mult)
            weights = PRB[:, 0:k, 0:H].unsqueeze(3).to_broadcast([P, k, H, F // H])
            v.tensor_tensor(PR[:, 0:k, :].rearrange("p k (h d) -> p k h d", h=H),
                            rows.rearrange("p k (h d) -> p k h d", h=H), weights, ALU.mult)
            if l == 0:
                v.scalar_tensor_tensor(NLU[:, t, 0:k], VB[:, t, 0:k], -2.0 * N / BIG, G[:, b, 0:k, T_AUX],
                                       ALU.mult, ALU.add)
            dve.drain()
            if run[0] < QUADS - 1:
                v.tensor_copy(IX[:, b, :], NLU[:, t + 4, :]).then_inc(ix_staged, 1)
            elif l < 3:
                v.tensor_copy(IX[:, b, :], NLU[:, b, :]).then_inc(ix_staged, 1)
            v.tensor_reduce(ACC, PR[:, 0:k, :].rearrange("p k f -> p f k"), AX.X, ALU.add)
            if l != 1:
                v.tensor_scalar(HH, MEAN[:], D0[:, t:t + 1] if type(t) is int else D0[:, bass.ds(t, 1)],
                                None, ALU.mult)
            dve.drain()
            if H > 1:
                heads = lambda ap: ap.rearrange("p (h d) -> p h d", h=H)
                v.tensor_tensor(heads(ACC), heads(ACC), RZ[:, 0:H].unsqueeze(2).to_broadcast([P, H, F // H]),
                                ALU.mult)
                dve.drain()
                v.tensor_tensor(HH, HH, ACC, ALU.add)
            else:
                v.scalar_tensor_tensor(HH, ACC, RZ[:, 0:1], TBL[:, t, 0:F] if l == 1 else HH, ALU.mult, ALU.add)
            dve.drain()
            v.tensor_scalar(EN, HH, 0.0, None, ALU.min).then_inc(en_made, 1)
            v.scalar_tensor_tensor(ACC, HH, 0.0, REC[:, t, 0:F], ALU.max, ALU.add)
            dve.drain()
            dve.wait_ge(ex_made, no + 1)
            if l < 3:
                v.scalar_tensor_tensor(REC[:, t, 0:F], EX, -1.0, ACC, ALU.add, ALU.add)
                dve.drain()
                norm(REC[:, t, 0:F], t, T + no, b % 2)
                if b == 3:
                    deviations(dve, v, 4 * q, 4)
            else:
                if run[0] > 0:
                    dve.wait_ge(ox_stored[b], 16 * q)
                v.tensor_copy(IDU[:, b:b + 1], REC[:, t, R_ID:R_ID + 1])
                v.scalar_tensor_tensor(OX[:, b, :], EX, -1.0, ACC, ALU.add, ALU.add).then_inc(ox_made, 1)

        def dense(dve, v, norm):
            for inst, (l, h) in enumerate(INST):
                D = F // HEADS[l]
                if h == 0:
                    layer_mean(dve, v, l)
                v.tensor_copy(X_TC, TBL[:, :, T_T + h])
                if l == 1:
                    v.tensor_scalar(X_TG, TBL[:, :, T_AUX], 0.0, 1.0, ALU.not_equal, ALU.subtract)
                    dve.drain()
                    v.scalar_tensor_tensor(X_TC, X_TG, BIG, X_TC, ALU.mult, ALU.add)
                dve.drain()
                with dve.Fori(0, T // 2) as i:
                    for b in range(2):
                        dve.wait_ge(x_tb, inst * T + 2 * i + b)
                        v.tensor_scalar(X_DIAG[:, b, :], IDN[:], X_TC[:, bass.ds(2 * i + b, 1)], None, ALU.mult
                                        ).then_inc(x_diag, 1)
                dve.wait_ge(x_tbc, (inst + 1) * T)
                with dve.Fori(0, T) as t:
                    no = inst * T + t
                    v.memset(X_M[:, 3:4], 0.0).then_inc(x_adj_free, 1)
                    dve.wait_ge(x_adj, 16 * no + 16)
                    v.tensor_scalar(X_BIAS, X_ADJ, 0.0, 1.0, ALU.is_gt, ALU.subtract)
                    v.tensor_scalar(X_E, X_T, TBL[:, t, T_S + h:T_S + h + 1], None, ALU.add)
                    dve.drain()
                    v.scalar_tensor_tensor(X_E, X_E, ALPHA, X_E, ALU.mult, ALU.max)
                    dve.drain()
                    v.scalar_tensor_tensor(X_E, X_BIAS, BIG, X_E, ALU.mult, ALU.add)
                    dve.drain()
                    v.tensor_reduce(X_M[:, 0:1], X_E, AX.X, ALU.max)
                    if l == 1:
                        v.tensor_scalar(X_BIAS, X_E, FLOOR, None, ALU.is_gt)
                        dve.drain()
                        v.tensor_reduce(X_M[:, 3:4], X_BIAS, AX.X, ALU.add)
                    dve.drain()
                    v.tensor_scalar(X_M[:, 1:2], X_M[:, 0:1], FLOOR, -1.0, ALU.max, ALU.mult).then_inc(x_sc, 1)
                    dve.wait_ge(x_exp, no + 1)
                    v.tensor_scalar(X_M[:, 4:5], X_M[:, 2:3], 1e-30, None, ALU.max)
                    v.tensor_scalar(X_M[:, 6:7], X_M[:, 2:3], 0.0, None, ALU.is_equal)
                    dve.drain()
                    v.reciprocal(X_M[:, 5:6], X_M[:, 4:5])
                    dve.drain()
                    if l == 1:
                        v.tensor_scalar(X_E, X_E, X_M[:, 5:6], None, ALU.mult)
                        dve.drain()
                        v.tensor_reduce(X_M[:, 7:8], X_E, AX.X, ALU.max)
                        v.scalar_tensor_tensor(X_E, X_E, THR, X_E, ALU.is_ge, ALU.mult)
                        dve.drain()
                        v.scalar_tensor_tensor(X_M[:, 5:6], X_M[:, 7:8], THR, X_M[:, 3:4], ALU.is_gt, ALU.mult)
                        dve.drain()
                        v.tensor_copy(X_H[:, 0:D], TBL[:, t, 0:D]).then_inc(x_pr, 1)
                    else:
                        v.tensor_scalar(X_H[:, 0:D], MEAN[:, h * D:(h + 1) * D], X_M[:, 6:7], None, ALU.mult
                                        ).then_inc(x_pr, 1)
                    dve.drain()
                    with dve.Fori(0, T // 8) as g:
                        for b in range(2):
                            dve.wait_ge(x_tr, no * (T // 4) + 2 * g + b)
                            v.tensor_copy(X_ST[:, b, :], X_E[:, bass.ds(g * (8 * P) + b * (4 * P), 4 * P)]
                                          ).then_inc(x_stg, 1)
                    dve.wait_ge(x_acc, no + 1)
                    v.scalar_tensor_tensor(X_H[:, 0:D], psM[1][:, 0:D], X_M[:, 5:6], X_H[:, 0:D], ALU.mult, ALU.add)
                    dve.drain()
                    x_rows = REC[:, t, h * D:(h + 1) * D]
                    v.scalar_tensor_tensor(x_rows, X_H[:, 0:D], 0.0, x_rows, ALU.max, ALU.add)
                    v.tensor_scalar(X_H[:, 0:D], X_H[:, 0:D], 0.0, None, ALU.min).then_inc(x_en, 1)
                    dve.drain()
                    dve.wait_ge(x_ex, no + 1)
                    v.scalar_tensor_tensor(x_rows, X_E1[:, 0:D], -1.0, x_rows, ALU.add, ALU.add)
                    dve.drain()
                if h == HEADS[l] - 1 and l < 3:
                    with dve.Fori(0, T // 2) as i:
                        for b in range(2):
                            norm(REC[:, 2 * i + b, 0:F], 2 * i + b, T * (l + 1) + 2 * i + b, b)
                    deviations(dve, v, 0, T)
            v.memset(X_M[:, 0:1], 0.0).then_inc(x_out, 1)

        @block.sync
        def _(sp):
            sp.dma_start(REC[:, :, 0:F], x.rearrange("(t p) f -> p t f", p=P)).then_inc(x_loaded, 16)
            for l in range(4):
                sp.dma_start(WA[:, l, 0:F], Ws[l]).then_inc(w_loaded, 16)
            sp.wait_ge(av_zeroed, 1)
            for l in (0, 1, 3):
                sp.dma_start(AV[:, l, 4:5], As[l][0:F, :]).then_inc(w_loaded, 16)
                sp.dma_start(AV[:, l, 0:1], As[l][F:2 * F, :]).then_inc(w_loaded, 16)
            D = F // 4
            for h in range(4):
                sp.dma_start(AV[h * D:(h + 1) * D, 2, 4 + h:5 + h],
                             As[2][0, h, 0:D].rearrange("(d a) -> d a", a=1)).then_inc(w_loaded, 16)
                sp.dma_start(AV[h * D:(h + 1) * D, 2, h:h + 1],
                             As[2][0, h, D:2 * D].rearrange("(d a) -> d a", a=1)).then_inc(w_loaded, 16)

            def load_adj(t, half, b):
                sp.dma_start(AREA[:, b, :], adj[bass.ds(t * P, P), half * HALF:(half + 1) * HALF]
                             ).then_inc(adj_loaded[b], 16)

            for h in range(4):
                load_adj(h // 2, h % 2, h)
            with sp.Fori(1, T // 2) as i:
                for h in range(4):
                    sp.wait_ge(mask_made, 4 * i + h - 3)
                    load_adj(2 * i + h // 2, h % 2, h)

            sp.wait_ge(rank_ready, 1)
            sp.dma_start(tab_d[0].rearrange("(t p) w -> p t w", p=P), TBL[:]).then_inc(table_stored, 16)
            sp.wait_ge(flag_ready, 1)
            overflow = sp.value_load(FLAGI[0:1, 0:1])
            with sp.If(overflow == 0):
                sp.wait_ge(rec_scattered, 16 * T)
                sp.dma_start(REC[:], rec_d.rearrange("(t p) w -> p t w", p=P)).then_inc(rec_loaded, 16)
                for l in range(3):
                    view = tab_d[l + 1].rearrange("(q j p) w -> q p j w", p=P, j=4)
                    with sp.Fori(0, QUADS) as q:
                        sp.wait_ge(tb_made, T * (l + 1) + 4 * q + 4)
                        sp.dma_start(view[q], TBL[:, bass.ds(4 * q, 4), :]).then_inc(table_stored, 16)
                for b in range(4):
                    sp.wait_ge(ox_stored[b], 16 * QUADS)
            with sp.Else():
                for inst in range(len(INST)):
                    with sp.Fori(0, T) as t:
                        sp.wait_ge(x_adj_free, inst * T + t + 1)
                        sp.dma_start(X_ADJ, adj[bass.ds(t * P, P), :]).then_inc(x_adj, 16)
                sp.wait_ge(x_out, 1)
                sp.dma_start(out.rearrange("(t p) f -> p t f", p=P), REC[:, :, 0:F]).then_inc(x_stored, 16)
                sp.wait_ge(x_stored, 16)

        def scatter(pool, bound, q, b):
            if type(q) is int and q == 0 and b < 2:
                return
            scatter_one(pool, bound, 4 * q + b - 2, (b - 2) % 4)

        def scatter_one(pool, bound, tile, b):
            pool.wait_ge(ox_made, tile + 1)
            pool.nop(nofuse=True)
            pool.indirect_dma_start(out, bass.IndirectOffsetOnAxis(ap=IDU[:, b:b + 1], axis=0),
                                    OX[:, b, :], None, bounds_check=bound, oob_is_err=False,
                                    ).then_inc(ox_stored[b], 16)

        @block.gpsimd
        def _(pool):
            bound = pool.to_reg(N - 1)
            nc.gpsimd.memset(IDN[:], 0.0).then_inc(iotas, 1)
            nc.gpsimd.memset(ONE[:], 1.0).then_inc(iotas, 1)
            pool.wait_ge(iotas, 2)
            nc.gpsimd.affine_select(out=IDN[:], in_=IDN[:], compare_op=ALU.not_equal, fill=1.0, base=0,
                                    pattern=[[-1, P]], channel_multiplier=1).then_inc(iotas, 1)
            nc.gpsimd.iota(pair_code, pattern=[[2, N // 2]], base=ODD0, channel_multiplier=0,
                           ).then_inc(iotas, 1)
            nc.gpsimd.affine_select(out=X_DIAG[:, 0, :], in_=ONE[:], compare_op=ALU.is_gt, fill=0.0, base=0,
                                    pattern=[[1, P]], channel_multiplier=-1).then_inc(upper_made, 1)
            nc.gpsimd.iota(RANKU[:], pattern=[[P, T]], base=0, channel_multiplier=1).then_inc(iotas, 1)

            pool.wait_ge(flag_ready, 1)
            overflow = pool.value_load(FLAGI[0:1, 0:1])
            with pool.If(overflow == 0):
                for t in range(T):
                    pool.indirect_dma_start(rec_d, bass.IndirectOffsetOnAxis(ap=RANKU[:, t:t + 1], axis=0),
                                            REC[:, t, :], None, bounds_check=bound, oob_is_err=False,
                                            ).then_inc(rec_scattered, 16)
                for l in range(4):
                    pool.wait_ge(table_stored, 16 * (1 + l * QUADS))
                    for run in RUNS:
                        for q in over(pool, run):
                            for b in range(4):
                                k = slots_of(run[0], b)
                                pool.wait_ge(ix_staged, l * T + 4 * q + b + 1)
                                pool.nop(nofuse=True)
                                for s in range(k):
                                    pool.indirect_dma_start(
                                        G[:, b, s, :], None, tab_d[l],
                                        bass.IndirectOffsetOnAxis(ap=IX[:, b, s:s + 1], axis=0),
                                        bounds_check=bound, oob_is_err=False).then_inc(gathered[b], 16)
                                if l == 3:
                                    scatter(pool, bound, q, b)
                for j in range(2):
                    scatter_one(pool, bound, T - 2 + j, 2 + j)

        @block.tensor
        def _(pe):
            pe.wait_ge(w_loaded, 16 * 18)
            pe.wait_ge(iotas, 3)
            for l in range(4):
                nc.tensor.transpose(psT[0][:, 0:P], WA[:, l, 0:F], IDN[:]).then_inc(wt_made, 1)
                pe.wait_ge(wt_copied, l + 1)
                nc.tensor.matmul(psW[0][:, 0:8], WT[:], AV[:, l, :], start=True, stop=True).then_inc(wa_made, 1)
                pe.wait_ge(wa_copied, l + 1)

            def project(l, tile_no, b):
                pe.wait_ge(hn_made, tile_no + 1)
                nc.tensor.transpose(psT[b][:, 0:P], HN[:, b, :], IDN[:]).then_inc(ht_psum, 1)
                pe.wait_ge(ht_made, tile_no + 1)
                if not (type(tile_no) is int and tile_no < 2):
                    pe.wait_ge(raw_kept, tile_no - 1)
                nc.tensor.matmul(psW[b][:, 0:TW], HT[:, b, :], WA[:, l, :], start=True, stop=True
                                 ).then_inc(wh_made, 1)

            def average(l, t, first, last):
                pe.wait_ge(tb_made, T * l + t + 1)
                nc.tensor.matmul(psM[l % 2][:, 0:F], ONEN[:], TBL[:, t, 0:F], start=first, stop=last,
                                 skip_group_check=True).then_inc(mean_made, 1)

            def project_all(l):
                for t in range(2):
                    project(l, T * l + t, t)
                with pe.Fori(1, T // 2) as i:
                    for b in range(2):
                        project(l, T * l + 2 * i + b, b)
                average(l, 0, True, False)
                with pe.Fori(1, T - 1) as t:
                    average(l, t, False, False)
                average(l, T - 1, False, True)

            pe.wait_ge(consts, 1)
            project_all(0)

            pe.wait_ge(onehot_made, 1)
            flat = OHB.rearrange("p c t -> p (c t)")
            n = NC * T
            for i, c in enumerate(range(0, n, 512)):
                w = min(512, n - c)
                dst = (psT[0], psT[1], psW[0])[i]
                nc.tensor.matmul(dst[:, 0:w], UPPER, flat[:, c:c + w], start=True, stop=True).then_inc(prefix_made, 1)
            for i, c in enumerate(range(0, n, 512)):
                w = min(512, n - c)
                dst = (psX[0], psX[1], psW[1])[i]
                nc.tensor.matmul(dst[:, 0:w], ONEB, flat[:, c:c + w], start=True, stop=True).then_inc(prefix_made, 1)
            pe.wait_ge(miss_made, 1)
            nc.tensor.matmul(psM[1][:, 0:1], ONE[:], FLAG[:, 0:1], start=True, stop=True).then_inc(flag_summed, 1)
            pe.wait_ge(flag_ready, 1)
            overflow = pe.value_load(FLAGI[0:1, 0:1])
            with pe.If(overflow == 0):
                for l in range(1, 4):
                    for run in RUNS:
                        for q in over(pe, run):
                            for j in range(4):
                                project(l, T * l + 4 * q + j, j % 2)
                            for j in range(4):
                                average(l, 4 * q + j, run[0] == 0 and j == 0, run[0] == QUADS - 1 and j == 3)
            with pe.Else():
                for inst, (l, h) in enumerate(INST):
                    D = F // HEADS[l]
                    with pe.Fori(0, T // 2) as i:
                        for b in range(2):
                            n = inst * T + 2 * i + b
                            pe.wait_ge(x_diag, n + 1)
                            nc.tensor.matmul(psX[b][:, 0:P], ONE[:], X_DIAG[:, b, :], start=True, stop=True
                                             ).then_inc(x_tb, 1)
                            pe.wait_ge(x_tbc, n + 1)
                    with pe.Fori(0, T) as t:
                        no = inst * T + t
                        pe.wait_ge(x_pr, no + 1)
                        nc.tensor.matmul(psM[1][:, 0:D], ZERO[:], ZERO[:, 0:D], start=True, stop=False,
                                         skip_group_check=True)
                        with pe.Fori(0, T // 8) as g:
                            for b in range(2):
                                pe.wait_ge(x_stg, no * (T // 4) + 2 * g + b + 1)
                                for c in range(4):
                                    tr = nc.tensor.transpose(psX[b][:, c * P:(c + 1) * P],
                                                             X_ST[:, b, c * P:(c + 1) * P], IDN[:])
                                tr.then_inc(x_tr, 1)
                                pe.wait_ge(x_trc, no * (T // 4) + 2 * g + b + 1)
                                for c in range(4):
                                    nc.tensor.matmul(psM[1][:, 0:D], X_PT[:, b, c * P:(c + 1) * P],
                                                     TBL[:, 8 * g + 4 * b + c, h * D:(h + 1) * D],
                                                     start=False, stop=False, skip_group_check=True)
                        nc.tensor.matmul(psM[1][:, 0:D], ZERO[:], ZERO[:, 0:D], start=False, stop=True,
                                         skip_group_check=True).then_inc(x_acc, 1)
                    if h == HEADS[l] - 1 and l < 3:
                        project_all(l + 1)

        @block.scalar
        def _(act):
            for l in range(4):
                act.wait_ge(wt_made, l + 1)
                nc.scalar.activation(WT[:], psT[0][:, 0:P], ACT.Copy).then_inc(wt_copied, 1)
                act.wait_ge(wa_made, l + 1)
                nc.scalar.activation(WA[:, l, F:TW], psW[0][:, 0:8], ACT.Copy).then_inc(wa_copied, 1)

            def rectify(no, b):
                act.wait_ge(ht_psum, no + 1)
                nc.scalar.activation(HT[:, b, :], psT[b][:, 0:P], ACT.Relu).then_inc(ht_made, 1)

            def keep(t, no, b):
                act.wait_ge(wh_made, no + 1)
                nc.scalar.activation(TBL[:, t, :], psW[b][:, 0:TW], ACT.Copy).then_inc(raw_kept, 1)

            def scale(t):
                nc.scalar.activation(TBL[:, t, :], TBL[:, t, :], ACT.Copy, scale=RSTD[:, bass.ds(t, 1)]
                                     ).then_inc(tb_made, 1)

            act.wait_ge(consts, 1)

            def extract(i, t, j):
                for half in range(2):
                    h = 2 * j + half
                    act.wait_ge(adj_loaded[h], 16 * i + 16)
                    if not (type(i) is int and i == 0 and h < 2):
                        act.wait_ge(mask_read, 4 * i + h - 1)
                    nc.scalar.activation(mask[:, half, :], AREA[:, h, :], ACT.Sigmoid, bias=C100[:],
                                         scale=200.0, accum_out=DEGH[:, bass.ds(2 * t + half, 1)]
                                         ).then_inc(mask_made, 1)
                rectify(t, j)
                keep(t, t, j)

            for j in range(2):
                extract(0, j, j)
            with act.Fori(1, T // 2) as i:
                for j in range(2):
                    extract(i, 2 * i + j, j)

            act.wait_ge(raw_kept, T)
            act.wait_ge(rstd_made, 1)
            with act.Fori(0, T) as t:
                scale(t)

            act.wait_ge(flag_ready, 1)
            overflow = act.value_load(FLAGI[0:1, 0:1])
            with act.If(overflow == 0):
                for l in range(4):
                    H = HEADS[l]
                    for run in RUNS:
                        for q in over(act, run):
                            for b in range(4):
                                k = slots_of(run[0], b)
                                no = l * T + 4 * q + b
                                act.wait_ge(sc_made, no + 1)
                                nc.scalar.activation(PRB[:, 0:k, 0:H], SCO[:, SLOTS - k:SLOTS, 0:H], ACT.Exp
                                                     ).then_inc(exp_made, 1)
                                act.wait_ge(en_made, no + 1)
                                nc.scalar.activation(EX, EN, ACT.Exp).then_inc(ex_made, 1)
                                if l < 3:
                                    rectify(T + no, b % 2)
                                    keep(4 * q + b, T + no, b % 2)
                            if l < 3:
                                act.wait_ge(raw_kept, T * (l + 1) + 4 * q + 4)
                                act.wait_ge(rstd_made, 2 + l * QUADS + q)
                                for b in range(4):
                                    scale(4 * q + b)
            with act.Else():
                for inst, (l, h) in enumerate(INST):
                    D = F // HEADS[l]
                    with act.Fori(0, T // 2) as i:
                        for b in range(2):
                            act.wait_ge(x_tb, inst * T + 2 * i + b + 1)
                            nc.scalar.activation(X_T[:, bass.ds(i * (2 * P) + b * P, P)], psX[b][:, 0:P], ACT.Copy
                                                 ).then_inc(x_tbc, 1)
                    with act.Fori(0, T) as t:
                        no = inst * T + t
                        act.wait_ge(x_sc, no + 1)
                        nc.scalar.activation(X_E, X_E, ACT.Exp, bias=X_M[:, 1:2], accum_out=X_M[:, 2:3]
                                             ).then_inc(x_exp, 1)
                        with act.Fori(0, T // 8) as g:
                            for b in range(2):
                                act.wait_ge(x_tr, no * (T // 4) + 2 * g + b + 1)
                                nc.scalar.activation(X_PT[:, b, :], psX[b][:], ACT.Copy).then_inc(x_trc, 1)
                        act.wait_ge(x_en, no + 1)
                        nc.scalar.activation(X_E1[:, 0:D], X_H[:, 0:D], ACT.Exp).then_inc(x_ex, 1)
                    if h == HEADS[l] - 1 and l < 3:
                        with act.Fori(0, T // 2) as i:
                            for b in range(2):
                                rectify(T * (l + 1) + 2 * i + b, b)
                                keep(2 * i + b, T * (l + 1) + 2 * i + b, b)
                        act.wait_ge(raw_kept, T * (l + 2))
                        act.wait_ge(rstd_made, 2 + l)
                        with act.Fori(0, T) as t:
                            scale(t)

        @block.vector
        def _(dve):
            v = nc.vector

            v.memset(AV[:], 0.0)
            dve.drain()
            v.memset(AV[:, 1, 1:2], 1.0).then_inc(av_zeroed, 1)
            v.memset(ONEN[:], 1.0 / N)
            v.memset(ZERO[:], 0.0)
            v.memset(C100[:], -100.0).then_inc(consts, 1)
            dve.wait_ge(x_loaded, 16)
            dve.wait_ge(iotas, 5)
            v.tensor_copy(REC[:, :, R_ID], RANKU[:])
            v.memset(REC[:, :, R_ID + 1:RW], 0.0)

            def norm(rows, t, no, b):
                v.bn_stats(ST[:, b, :], rows)
                dve.drain()
                v.bn_aggr(MV[:, b, :], ST[:, b, :])
                dve.drain()
                v.tensor_scalar(VAR[:, bass.ds(t, 1)], MV[:, b, 1:2], EPS, None, ALU.add)
                if not (type(no) is int and no < 2):
                    dve.wait_ge(ht_psum, no - 1)
                v.tensor_scalar(HN[:, b, :], rows, MV[:, b, 0:1], None, ALU.subtract).then_inc(hn_made, 1)

            def extract(i, t, j):
                for half in range(2):
                    dve.wait_ge(mask_made, 4 * i + 2 * j + half + 1)
                    v.tensor_tensor(code[:, half, :], mask[:, half, :].bitcast(U16),
                                    pair_code[:, half * HP:(half + 1) * HP], ALU.mult).then_inc(mask_read, 1)
                    dve.drain()
                    for s in range(SEGS):
                        at = (half * SEGS + s) * 8
                        v.max(CND[:, at:at + 8], code[:, half, s * SEG:(s + 1) * SEG])
                norm(REC[:, t, 0:F], t, t, j)
                dve.drain()
                v.max(TOP[:, 0:8], CND[:])
                dve.drain()
                v.match_replace(CND2[:], TOP[:, 0:8], CND[:], 0.0)
                dve.drain()
                v.max(TOP[:, 8:16], CND2[:])
                dve.drain()
                v.tensor_copy(CODES[:, t, :], TOP[:])

            for j in range(2):
                extract(0, j, j)
            with dve.Fori(1, T // 2) as i:
                for j in range(2):
                    extract(i, 2 * i + j, j)
            deviations(dve, v, 0, T)
            dve.drain()

            c = CODES[:].rearrange("p t s -> p (t s)")
            v.tensor_copy(D_I, c)
            v.tensor_scalar(D_B, c, 32768.0, None, ALU.is_ge)
            dve.drain()
            v.tensor_scalar(D_I, D_I, 1, None, ALU.bitwise_and)
            dve.drain()
            v.tensor_copy(D_ODD, D_I)
            dve.drain()
            v.tensor_scalar(D_W, D_ODD, 1 / 256 - 1 / 257, 1 - 1 / 256, ALU.mult, ALU.add)
            dve.drain()
            v.tensor_tensor(D_W, D_W, D_B, ALU.mult)
            dve.drain()
            v.tensor_scalar(D_W, D_W, -1.0, 1.0, ALU.mult, ALU.add)
            dve.drain()
            v.tensor_tensor(D_Q, c, D_W, ALU.mult)
            dve.drain()
            ROUND = 12582912.0
            v.tensor_scalar(D_Q, D_Q, ROUND, None, ALU.add)
            dve.drain()
            v.tensor_scalar(D_Q, D_Q, ROUND, None, ALU.subtract)
            dve.drain()
            three = lambda ap: ap.rearrange("p (t s) -> p t s", t=T)
            v.scalar_tensor_tensor(L32[:, :, 0:SLOTS], three(D_Q), float(-(ODD0 - 1)), three(D_ODD),
                                   ALU.add, ALU.mult)
            v.scalar_tensor_tensor(L32[:, :, SLOTS:], three(D_Q), float(-(ODD0 - 2)), three(D_B),
                                   ALU.add, ALU.mult)
            dve.drain()
            v.tensor_scalar(TMP, L32, 0.0, None, ALU.is_gt)
            dve.drain()
            v.tensor_reduce(COUNT[:], TMP, AX.X, ALU.add)

            with dve.Fori(0, QUADS) as q:
                v.tensor_copy(S32, L32[:, bass.ds(4 * q, 4), :])
                dve.drain()
                for j in range(4):
                    v.max(S16[:, j, 0:8], S32[:, j, :])
                dve.drain()
                for j in range(4):
                    v.match_replace(S32B[:, j, :], S16[:, j, 0:8], S32[:, j, :], 0.0)
                dve.drain()
                for j in range(4):
                    v.max(S16[:, j, 8:16], S32B[:, j, :])
                dve.drain()
                v.tensor_copy(REC[:, bass.ds(4 * q, 4), R_NL:R_NL + SLOTS], S16)
                dve.drain()

            for k in range(NC):
                v.memset(CLS[:, k, :], float(SLOTS - k))
            v.memset(ONEB, 1.0)
            dve.wait_ge(upper_made, 1)
            v.tensor_copy(UPPER, X_DIAG[:, 0, :])
            dve.drain()
            cnt = COUNT[:].unsqueeze(1).to_broadcast([P, NC, T])
            v.tensor_tensor(OH, CLS, cnt, ALU.is_equal)
            dve.drain()
            v.tensor_copy(OHB, OH).then_inc(onehot_made, 1)
            v.tensor_tensor(MIS, DEGH[:, 0:2 * T:2], DEGH[:, 1:2 * T:2], ALU.add)
            dve.drain()
            v.tensor_scalar(MIS, MIS, 0.5, None, ALU.subtract)
            dve.drain()
            v.tensor_tensor(MIS, MIS, COUNT[:], ALU.is_gt)
            v.tensor_scalar(TMP[:, 0:2, :].rearrange("p a b -> p (a b)"), COUNT[:], SLOTS + 0.5, None, ALU.is_gt)
            dve.drain()
            v.tensor_tensor(MIS, MIS, TMP[:, 0:2, :].rearrange("p a b -> p (a b)"), ALU.add)
            dve.drain()
            v.tensor_reduce(FLAG[:, 0:1], MIS, AX.X, ALU.add)

            def bank(i):
                return i * 512, min(512, NC * T - i * 512)

            tot = TOT.rearrange("p c t -> p (c t)")
            dve.wait_ge(prefix_made, 6)
            for i, src in enumerate((psX[0], psX[1], psW[1])):
                at, w = bank(i)
                v.tensor_copy(tot[:, at:at + w], src[:, 0:w])
            dve.drain()
            src, step, n = TOT, 1, 0
            while step < T:
                dst = SC[n % 2]
                v.tensor_tensor(dst[:, :, step:], src[:, :, step:], src[:, :, :T - step], ALU.add)
                v.tensor_copy(dst[:, :, 0:step], src[:, :, 0:step])
                dve.drain()
                src, step, n = dst, 2 * step, n + 1
            run_t, other = src, SC[n % 2]
            v.memset(CT[0][:, 0:1], 0.0)
            v.tensor_copy(CT[0][:, 1:NC + 1], run_t[:, :, T - 1])
            dve.drain()
            m, step = 0, 1
            while step < NC + 1:
                v.tensor_tensor(CT[1 - m][:, step:], CT[m][:, step:], CT[m][:, :NC + 1 - step], ALU.add)
                v.tensor_copy(CT[1 - m][:, 0:step], CT[m][:, 0:step])
                dve.drain()
                m, step = 1 - m, 2 * step
            above = CT[m]
            for quad in range(QUADS):
                for j in range(4 if quad == 0 else 1):
                    k = slots_of(quad, j)
                    if k < SLOTS and not (quad > 1 and QUAD_SLOTS[quad - 2] == k):
                        v.tensor_scalar(FLAG[:, 1:2], above[:, SLOTS - k:SLOTS - k + 1],
                                        P * (4 * quad + j) + 0.5, None, ALU.is_gt)
                        dve.drain()
                        v.tensor_tensor(FLAG[:, 0:1], FLAG[:, 0:1], FLAG[:, 1:2], ALU.add)
                        dve.drain()
            v.tensor_scalar(FLAG[:, 2:3], FLAG[:, 0:1], 1.0, None, ALU.mult).then_inc(miss_made, 1)
            v.tensor_tensor(other, run_t, TOT, ALU.subtract)
            dve.drain()
            v.tensor_tensor(other, other, above[:, 0:NC].unsqueeze(2).to_broadcast([P, NC, T]), ALU.add)
            dve.drain()
            flat = other.rearrange("p c t -> p (c t)")
            for i, src in enumerate((psT[0], psT[1], psW[0])):
                at, w = bank(i)
                v.tensor_tensor(flat[:, at:at + w], flat[:, at:at + w], src[:, 0:w], ALU.add)
            dve.drain()
            v.tensor_tensor(other, other, OH, ALU.mult)
            dve.drain()
            v.tensor_reduce(RANKF[:], other.rearrange("p c t -> p t c"), AX.X, ALU.add)
            dve.drain()
            v.tensor_copy(RANKU[:], RANKF[:])
            dve.wait_ge(tb_made, T)
            v.tensor_copy(TBL[:, :, T_AUX], RANKF[:])
            v.tensor_copy(REC[:, :, R_S:R_S + 4], TBL[:, :, T_S:T_S + 4])
            dve.wait_ge(mean_made, T)
            v.tensor_copy(MEAN[:], psM[0][:, 0:F]).then_inc(rank_ready, 1)
            dve.wait_ge(flag_summed, 1)
            v.tensor_copy(FLAGI[:], psM[1][:, 0:1]).then_inc(flag_ready, 1)
            dve.wait_ge(flag_ready, 1)
            overflow = dve.value_load(FLAGI[0:1, 0:1])
            with dve.If(overflow == 0):
                fast(dve, v, norm)
            with dve.Else():
                dense(dve, v, norm)


_INS = ["x", "adj", "L0_gnn_W", "L0_gnn_a", "L1_gnn_W", "L1_gnn_a", "L2_gnn_W", "L2_gnn_a",
        "L3_gnn_W", "L3_gnn_a"]
_OUTS = [((8192, 128), "float32")]


def kernel(**inputs):
    import numpy as _np
    import concourse.bacc as _bacc
    from concourse import mybir as _mybir
    from concourse.bass_utils import run_bass_kernel_spmd as _run

    nc = _bacc.Bacc("TRN2", target_bir_lowering=False, num_devices=1)
    arrays, args = {}, []
    for name in _INS:
        a = _np.ascontiguousarray(inputs[name])
        arrays[f"in_{name}_dram"] = a
        args.append(nc.dram_tensor(f"in_{name}_dram", a.shape, _mybir.dt.from_np(a.dtype), kind="ExternalInput").ap())
    for i, (shape, dtype) in enumerate(_OUTS):
        dt = _mybir.dt.from_np(_np.dtype(dtype))
        args.append(nc.dram_tensor(f"out_{i}_dram", shape, dt, kind="ExternalOutput").ap())
    gat_kernel(nc, *args)
    r = _run(nc, [arrays], core_ids=[0])
    return r.results[0]["out_0_dram"]
```

```python
from contextlib import ExitStack

import concourse.bass as bass
from concourse import mybir

ALU = mybir.AluOpType
ACT = mybir.ActivationFunctionType
AX = mybir.AxisListType
F32 = mybir.dt.float32
BF16 = mybir.dt.bfloat16
U8 = mybir.dt.uint8
U16 = mybir.dt.uint16
U32 = mybir.dt.uint32
I32 = mybir.dt.int32

P = 128
EPS = 1e-5
ALPHA = 0.2
THR = 1e-4
BIG = 2.0 ** 100
FLOOR = -2.0 ** 90
ROUND = 12582912.0
SLOTS = 16
HEADS = [1, 1, 4, 1]

FIRST_QUAD = [16, 9, 8, 8]
QUAD_SLOTS = [7, 6, 6, 5, 5, 5, 4, 4, 4, 3, 3, 3, 2, 2, 1]
QMAX = max(QUAD_SLOTS)
PAIR_RUNS = [(1, 2, 7), (5, 2, 5), (9, 2, 4), (13, 1, 2)]

R_S, R_NL, R_ID, RW = 128, 132, 148, 152
T_T, T_AUX, T_S, TW = 128, 129, 132, 136


def slots_of(quad, j):
    return FIRST_QUAD[j] if quad == 0 else QUAD_SLOTS[quad - 1]


def gat_kernel(nc, x, adj, W0, a0, W1, a1, W2, a2, W3, a3, out):
    N, F = x.shape
    T = N // P
    QUADS = T // 4
    HALF = N // 2
    HP = HALF // 2
    SEG = 512
    SEGS = HP // SEG
    CAND = 2 * SEGS * 8
    NC = SLOTS + 1
    NT = N + 1
    ODD0 = N + 1
    Ws, As = [W0, W1, W2, W3], [a0, a1, a2, a3]
    INST = [(l, h) for l in range(4) for h in range(HEADS[l])]

    rec_d = nc.dram_tensor("records_sorted", (N, RW), F32, kind="Internal").ap()
    tab_d = nc.dram_tensor("tables", (2 * NT, TW), F32, kind="Internal").ap()

    with ExitStack() as ctx:
        def sb(name, shape, dt):
            return ctx.enter_context(nc.sbuf_tensor(name, shape, dt))

        def sem(name):
            return ctx.enter_context(nc.semaphore(name))

        REC = sb("REC", [P, T, RW], F32)
        TBL = sb("TBL", [P, T, TW], F32)
        WA = sb("WA", [P, 4, TW], F32)
        WT = sb("WT", [P, P], F32)
        AV = sb("AV", [P, 4, 8], F32)
        IDN = sb("IDN", [P, P], F32)
        ONE = sb("ONE", [P, P], F32)
        ONEN = sb("ONEN", [P, P], F32)
        ZERO = sb("ZERO", [P, P], F32)
        MEAN = sb("MEAN", [P, F], F32)
        MEANR = sb("MEANR", [1, TW], F32)
        C100 = sb("C100", [P, 1], F32)
        ST = sb("ST", [P, 4, 6], F32)
        MV = sb("MV", [P, 4, 2], F32)
        NM = sb("NM", [P, 4], F32)
        VAR = sb("VAR", [P, T], F32)
        RSTD = sb("RSTD", [P, T], F32)
        NEWT = sb("NEWT", [P, T], F32)
        SEED = sb("SEED", [P, T], I32)
        HN = sb("HN", [P, 4, F], F32)
        HT = sb("HT", [P, 2, F], F32)
        NLU = sb("NLU", [P, T, SLOTS], U32)
        IDU = sb("IDU", [P, T], U32)
        DEGH = sb("DEGH", [P, 2 * T], F32)
        DEG = sb("DEG", [P, T], F32)
        RANKF = sb("RANKF", [P, T], F32)
        RANKU = sb("RANKU", [P, T], U32)
        FLAG = sb("FLAG", [P, 4], F32)
        FLAGI = sb("FLAGI", [P, 1], I32)

        AREA = sb("AREA", [P, 4, HALF], I32)
        AREB = sb("AREB", [P, 8192], F32)
        AREC = sb("AREC", [P, 3712], F32)
        area = AREA[:].rearrange("p a b -> p (a b)")

        def part(base, shape, dt=F32, of=None):
            n = 1
            for s in shape:
                n *= s
            of = area if of is None else of
            v = of[:, base:base + (n if dt in (F32, U32, I32) else n // 2)]
            if dt is not of.dtype:
                v = v.bitcast(dt)
            names = "abcd"[:len(shape)]
            if len(shape) == 1:
                return v
            return v.rearrange(f"p ({' '.join(names)}) -> p {' '.join(names)}",
                               **dict(zip(names, shape)))

        def part_c(base, shape, dt=F32):
            return part(base, shape, dt, AREC[:])

        mask = AREB[:, 0:2048].bitcast(U8).rearrange("p (b n) -> p b n", b=2)
        pair_code = AREB[:, 2048:4096].bitcast(U16)
        code = AREB[:, 4096:8192].rearrange("p (b n) -> p b n", b=2)
        CND = part_c(0, [2, CAND])
        CND2 = part_c(128, [CAND])
        TOP = part_c(192, [4, SLOTS])
        CQ = part_c(256, [4, SLOTS])
        D_R = part_c(320, [4, SLOTS])
        D_T = part_c(384, [4, SLOTS])
        D_ODD = part_c(448, [4, SLOTS])
        D_B = part_c(512, [4, SLOTS])
        D_W = part_c(576, [4, SLOTS])
        D_Q = part_c(640, [4, SLOTS])
        L32 = part_c(704, [4, 2 * SLOTS])
        S32 = part_c(832, [4, 2 * SLOTS])
        S16 = part_c(960, [4, SLOTS])
        UPPERF = part_c(1024, [P])

        CLS = part(0, [NC, T])
        OH = part(1152, [NC, T])
        OHB = part(2304, [NC, T], BF16)
        TOT = part(2944, [NC, T])
        SC = [part(4096, [NC, T]), part(5248, [NC, T])]
        CT = [part(6400, [NC + 1]), part(6432, [NC + 1])]
        UPPER = part(6464, [P], BF16)
        ONEB = part(6528, [P], BF16)
        CNT = part(6592, [T])
        MIS = part(6656, [T])
        VALID = part(6720, [T, SLOTS])
        DCAP = part(7744, [T])

        G0 = part(0, [4, SLOTS, TW])
        GQ = [part(8704 + b * 4 * QMAX * TW, [4, QMAX, TW]) for b in range(2)]
        PR = AREB[:]
        VB = part_c(0, [T, SLOTS])
        SCO = part_c(1024, [4 * SLOTS * 4])
        PRB = part_c(1280, [4 * SLOTS * 4])
        AUX1 = part_c(1536, [4 * SLOTS])
        AUX2 = part_c(1600, [4 * SLOTS])
        MX = part_c(1664, [16])
        Z = part_c(1680, [16])
        RZ = part_c(1696, [16])
        LCNT = part_c(1712, [4])
        TOPA = part_c(1716, [4])
        HH = part_c(1728, [4, F])
        POS = part_c(2240, [4, F])
        NEG = part_c(2752, [4, F])
        EX = sb("EX", [P, 4, F], F32)

        X_ADJ = part(0, [N], I32)
        X_BIAS = part(0, [N])
        X_E = part(N, [N])
        X_T = AREB[:, 0:N]
        X_TC = part_c(0, [T])
        X_TG = part_c(64, [T])
        X_DIAG = part_c(128, [2, P])
        X_ST = part_c(384, [2, 4 * P])
        X_PT = part_c(1408, [2, 4 * P])
        X_M = part_c(2432, [8])
        X_H = part_c(2440, [F])
        X_E1 = part_c(2568, [F])

        def ps(name):
            return ctx.enter_context(nc.psum_tensor(name, [P, 512], F32))

        psT = [ps("psT0"), ps("psT1")]
        psW = [ps("psW0"), ps("psW1"), ps("psX0"), ps("psX1")]
        psX = psW[2:]
        psM = [ps("psM0"), ps("psM1")]

        x_loaded = sem("x_loaded")
        w_loaded = sem("w_loaded")
        av_set = sem("av_set")
        consts = sem("consts")
        iotas = sem("iotas")
        wt_made = sem("wt_made")
        wt_copied = sem("wt_copied")
        wa_made = sem("wa_made")
        wa_copied = sem("wa_copied")
        adj_loaded = [sem(f"adj_loaded{b}") for b in range(4)]
        mask_made = sem("mask_made")
        mask_read = sem("mask_read")
        codes_ready = sem("codes_ready")
        codes_taken = sem("codes_taken")
        decoded = sem("decoded")
        lists_free = sem("lists_free")
        moments_made = sem("moments_made")
        hn_made = sem("hn_made")
        ht_psum = sem("ht_psum")
        ht_made = sem("ht_made")
        wh_made = sem("wh_made")
        raw_kept = sem("raw_kept")
        rstd_made = sem("rstd_made")
        tb_made = sem("tb_made")
        mean_made = sem("mean_made")
        meanrow_made = sem("meanrow_made")
        onehot_made = sem("onehot_made")
        prefix_made = sem("prefix_made")
        miss_made = sem("miss_made")
        flag_summed = sem("flag_summed")
        flag_ready = sem("flag_ready")
        rank_ready = sem("rank_ready")
        table_stored = sem("table_stored")
        rec_scattered = sem("rec_scattered")
        rec_loaded = sem("rec_loaded")
        lists_ready = sem("lists_ready")
        gathered = [sem("gathered_first"), sem("gathered_odd"), sem("gathered_even")]
        g_free = sem("g_free")
        sc_made = sem("sc_made")
        exp_made = sem("exp_made")
        h_made = sem("h_made")
        ex_made = sem("ex_made")
        x_final = sem("x_final")
        out_stored = sem("out_stored")
        upper_made = sem("upper_made")
        x_adj = sem("dense_adj_loaded")
        x_adj_free = sem("dense_adj_free")
        x_diag = sem("dense_diag_made")
        x_tb = sem("dense_t_spread")
        x_tbc = sem("dense_t_copied")
        x_sc = sem("dense_scores_made")
        x_exp = sem("dense_exp_made")
        x_pr = sem("dense_weights_ready")
        x_stg = sem("dense_block_staged")
        x_tr = sem("dense_transposed")
        x_trc = sem("dense_transposed_copied")
        x_acc = sem("dense_summed")
        x_en = sem("dense_en_made")
        x_ex = sem("dense_ex_made")
        x_out = sem("dense_out_made")
        x_stored = sem("dense_out_stored")

        block = ctx.enter_context(nc.Block())

        def landed_by(quad):
            if quad == 0:
                return 16 * sum(FIRST_QUAD)
            return sum(16 * 4 * slots_of(k, 0) for k in range(2 - quad % 2, quad + 1, 2))

        TABLE_DMAS = 16 * (QUADS + 1)

        @block.sync
        def _(sp):
            sp.dma_start(REC[:, :, 0:F], x.rearrange("(t p) f -> p t f", p=P)).then_inc(x_loaded, 16)

            def load_adj(t, h):
                sp.dma_start(AREA[:, h % 4, :], adj[bass.ds(t * P, P), (h % 2) * HALF:(h % 2 + 1) * HALF]
                             ).then_inc(adj_loaded[h % 4], 16)

            for h in range(4):
                load_adj(h // 2, h)
            for l in range(4):
                sp.dma_start(WA[:, l, 0:F], Ws[l]).then_inc(w_loaded, 16)
            sp.wait_ge(av_set, 1)
            for l in (0, 1, 3):
                sp.dma_start(AV[:, l, 4:5], As[l][0:F, :]).then_inc(w_loaded, 16)
                sp.dma_start(AV[:, l, 0:1], As[l][F:2 * F, :]).then_inc(w_loaded, 16)
            D = F // 4
            for h in range(4):
                sp.dma_start(AV[h * D:(h + 1) * D, 2, 4 + h:5 + h],
                             As[2][0, h, 0:D].rearrange("(d a) -> d a", a=1)).then_inc(w_loaded, 16)
                sp.dma_start(AV[h * D:(h + 1) * D, 2, h:h + 1],
                             As[2][0, h, D:2 * D].rearrange("(d a) -> d a", a=1)).then_inc(w_loaded, 16)
            with sp.Fori(1, T // 2) as i:
                for h in range(4):
                    sp.wait_ge(mask_made, 4 * i + h - 3)
                    load_adj(2 * i + h // 2, h)

            def table_rows(l, t, n):
                return tab_d[bass.ds(l % 2 * NT + t * P, n * P), :].rearrange("(t p) w -> p t w", p=P)

            def store_mean(l):
                sp.wait_ge(meanrow_made, l + 1)
                sp.dma_start(tab_d[l % 2 * NT + N:l % 2 * NT + NT, :], MEANR[:]).then_inc(table_stored, 16)

            sp.wait_ge(rank_ready, 1)
            sp.dma_start(table_rows(0, 0, T), TBL[:]).then_inc(table_stored, 16)
            sp.dma_start(table_rows(1, 0, T), TBL[:]).then_inc(table_stored, 16)
            store_mean(0)
            sp.dma_start(tab_d[NT + N:2 * NT, :], MEANR[:]).then_inc(table_stored, 16)
            sp.wait_ge(flag_ready, 1)
            overflow = sp.value_load(FLAGI[0:1, 0:1])
            with sp.If(overflow == 0):
                sp.wait_ge(rec_scattered, 16 * T)
                rec_v = rec_d.rearrange("(t p) w -> p t w", p=P)
                sp.dma_start(REC[:, 0:4, :], rec_v[:, 0:4, :]).then_inc(rec_loaded, 16)
                sp.wait_ge(rec_loaded, 16)
                sp.dma_start(REC[:, 4:T, :], rec_v[:, 4:T, :]).then_inc(rec_loaded, 16)
                for l in range(1, 4):
                    with sp.Fori(0, QUADS) as q:
                        sp.wait_ge(tb_made, T * l + 4 * q + 4)
                        sp.dma_start(table_rows(l, 4 * q, 4), TBL[:, bass.ds(4 * q, 4), :]
                                     ).then_inc(table_stored, 16)
                    store_mean(l)
                sp.wait_ge(out_stored, 16 * T)
            with sp.Else():
                for inst in range(len(INST)):
                    with sp.Fori(0, T) as t:
                        sp.wait_ge(x_adj_free, inst * T + t + 1)
                        sp.dma_start(X_ADJ, adj[bass.ds(t * P, P), :]).then_inc(x_adj, 16)
                sp.wait_ge(x_out, 1)
                sp.dma_start(out.rearrange("(t p) f -> p t f", p=P), REC[:, :, 0:F]).then_inc(x_stored, 16)
                sp.wait_ge(x_stored, 16)

        @block.gpsimd
        def _(pool):
            g = nc.gpsimd
            bound = pool.to_reg(2 * NT - 1)
            row_bound = pool.to_reg(N - 1)
            g.memset(IDN[:], 0.0).then_inc(iotas, 1)
            g.memset(ONE[:], 1.0).then_inc(iotas, 1)
            pool.wait_ge(iotas, 2)
            g.affine_select(out=IDN[:], in_=IDN[:], compare_op=ALU.not_equal, fill=1.0, base=0,
                            pattern=[[-1, P]], channel_multiplier=1).then_inc(iotas, 1)
            g.iota(pair_code, pattern=[[2, N // 2]], base=ODD0, channel_multiplier=0).then_inc(iotas, 1)
            g.affine_select(out=UPPERF, in_=ONE[:], compare_op=ALU.is_gt, fill=0.0, base=0,
                            pattern=[[1, P]], channel_multiplier=-1).then_inc(upper_made, 1)
            g.iota(RANKU[:], pattern=[[P, T]], base=0, channel_multiplier=1).then_inc(iotas, 1)

            def decode(i):
                pool.wait_ge(codes_ready, i + 1)
                pool.nop(nofuse=True)
                g.tensor_scalar(D_R, CQ, 0.5, ROUND, ALU.mult, ALU.add)
                g.tensor_scalar(D_B, CQ, 32768.0, None, ALU.is_ge)
                pool.drain()
                g.tensor_scalar(D_R, D_R, -ROUND, 2.0, ALU.add, ALU.mult)
                pool.drain()
                g.tensor_tensor(D_T, CQ, D_R, ALU.subtract)
                pool.drain()
                g.tensor_tensor(D_ODD, D_T, D_T, ALU.mult)
                pool.drain()
                g.tensor_scalar(D_W, D_ODD, 1 / 256 - 1 / 257, 1 - 1 / 256, ALU.mult, ALU.add)
                pool.drain()
                g.tensor_tensor(D_W, D_W, D_B, ALU.mult)
                pool.drain()
                g.tensor_scalar(D_W, D_W, -1.0, 1.0, ALU.mult, ALU.add)
                pool.drain()
                g.tensor_tensor(D_Q, CQ, D_W, ALU.mult).then_inc(codes_taken, 1)
                pool.drain()
                g.tensor_scalar(D_Q, D_Q, 1.0, ROUND, ALU.mult, ALU.add)
                pool.drain()
                g.tensor_scalar(D_R, D_Q, -ROUND, float(-(ODD0 - 1)), ALU.add, ALU.add)
                g.tensor_scalar(D_T, D_Q, -ROUND, float(-(ODD0 - 2)), ALU.add, ALU.add)
                pool.drain()
                pool.wait_ge(lists_free, i + 1)
                pool.nop(nofuse=True)
                g.tensor_tensor(L32[:, :, 0:SLOTS], D_R, D_ODD, ALU.mult)
                g.tensor_tensor(L32[:, :, SLOTS:], D_T, D_B, ALU.mult).then_inc(decoded, 1)

            with pool.Fori(0, QUADS) as i:
                decode(i)

            def gather_layer(l, last):
                pool.wait_ge(table_stored, TABLE_DMAS * l + 64)
                pool.nop(nofuse=True)
                for q in range(QUADS):
                    if q >= 3:
                        pool.wait_ge(g_free, QUADS * l + (q - 2) + 1)
                        pool.nop(nofuse=True)
                    landed = gathered[0 if q == 0 else 2 - q % 2]
                    for j in range(4):
                        for s in range(slots_of(q, j)):
                            t = 4 * q + j
                            dst = G0[:, j, s, :] if q == 0 else GQ[(q + 1) % 2][:, j, s, :]
                            pool.indirect_dma_start(
                                dst, None, tab_d, bass.IndirectOffsetOnAxis(ap=NLU[:, t, s:s + 1], axis=0),
                                bounds_check=bound, oob_is_err=False,
                            ).then_inc(landed, 16)
                    if last and q >= 2:
                        scatter_quad(q - 2)
                if last:
                    scatter_quad(QUADS - 2)
                    scatter_quad(QUADS - 1)

            def scatter_quad(q):
                pool.wait_ge(x_final, q + 1)
                for j in range(4):
                    t = 4 * q + j
                    pool.indirect_dma_start(out, bass.IndirectOffsetOnAxis(ap=IDU[:, t:t + 1], axis=0),
                                            REC[:, t, 0:F], None, bounds_check=row_bound, oob_is_err=False,
                                            ).then_inc(out_stored, 16)

            pool.wait_ge(flag_ready, 1)
            overflow = pool.value_load(FLAGI[0:1, 0:1])
            with pool.If(overflow == 0):
                for t in range(T):
                    pool.indirect_dma_start(rec_d, bass.IndirectOffsetOnAxis(ap=RANKU[:, t:t + 1], axis=0),
                                            REC[:, t, :], None, bounds_check=row_bound, oob_is_err=False,
                                            ).then_inc(rec_scattered, 16)
                pool.wait_ge(lists_ready, 1)
                with pool.Fori(0, 3) as l:
                    gather_layer(l, False)
                gather_layer(3, True)

        @block.tensor
        def _(pe):
            pe.wait_ge(w_loaded, 16 * 18)
            pe.wait_ge(iotas, 3)
            for l in range(4):
                nc.tensor.transpose(psT[0][:, 0:P], WA[:, l, 0:F], IDN[:]).then_inc(wt_made, 1)
                pe.wait_ge(wt_copied, l + 1)
                nc.tensor.matmul(psW[0][:, 0:8], WT[:], AV[:, l, :], start=True, stop=True).then_inc(wa_made, 1)
                pe.wait_ge(wa_copied, l + 1)

            def project(l, no, j, kept):
                pe.wait_ge(hn_made, no + 1)
                nc.tensor.transpose(psT[j % 2][:, 0:P], HN[:, j, :], IDN[:]).then_inc(ht_psum, 1)
                pe.wait_ge(ht_made, no + 1)
                if kept is not None:
                    pe.wait_ge(*kept)
                nc.tensor.matmul(psW[j][:, 0:TW], HT[:, j % 2, :], WA[:, l, :], start=True, stop=True
                                 ).then_inc(wh_made, 1)

            def project_quad(l, q):
                for j in range(4):
                    project(l, T * l + 4 * q + j, j, (tb_made, T * l + 4 * q))

            def average_quad(l, q):
                for j in range(4):
                    pe.wait_ge(tb_made, T * l + 4 * q + j + 1)
                    nc.tensor.matmul(psM[l % 2][:, 0:F], ONEN[:], TBL[:, 4 * q + j, 0:F],
                                     start=type(q) is int and q == 0 and j == 0,
                                     stop=type(q) is int and q == QUADS - 1 and j == 3,
                                     skip_group_check=True).then_inc(mean_made, 1)

            pe.wait_ge(consts, 1)
            for j in range(4):
                project(0, j, j, None)
            with pe.Fori(1, QUADS) as q:
                for j in range(4):
                    project(0, 4 * q + j, j, (raw_kept, 4 * q + j - 3))

            pe.wait_ge(raw_kept, T)
            pe.wait_ge(onehot_made, 1)
            flat = OHB.rearrange("p c t -> p (c t)")
            n = NC * T
            for i, c in enumerate(range(0, n, 512)):
                w = min(512, n - c)
                nc.tensor.matmul((psX[0], psX[1], psW[1])[i][:, 0:w], ONEB, flat[:, c:c + w], start=True, stop=True
                                 ).then_inc(prefix_made, 1)
            for i, c in enumerate(range(0, n, 512)):
                w = min(512, n - c)
                nc.tensor.matmul((psT[0], psT[1], psW[0])[i][:, 0:w], UPPER, flat[:, c:c + w], start=True, stop=True
                                 ).then_inc(prefix_made, 1)
            average_quad(0, 0)
            with pe.Fori(1, QUADS - 1) as q:
                average_quad(0, q)
            average_quad(0, QUADS - 1)
            pe.wait_ge(miss_made, 1)
            nc.tensor.matmul(psM[1][:, 0:1], ONE[:], FLAG[:, 0:1], start=True, stop=True).then_inc(flag_summed, 1)
            pe.wait_ge(flag_ready, 1)
            overflow = pe.value_load(FLAGI[0:1, 0:1])
            with pe.If(overflow == 0):
                for l in range(1, 4):
                    project_quad(l, 0)
                    average_quad(l, 0)
                    with pe.Fori(1, QUADS - 1) as q:
                        project_quad(l, q)
                        average_quad(l, q)
                    project_quad(l, QUADS - 1)
                    average_quad(l, QUADS - 1)
            with pe.Else():
                pe.nop(nofuse=True).then_inc(x_tb, 1)
                pe.nop(nofuse=True).then_inc(x_tr, 1)
                for inst, (l, h) in enumerate(INST):
                    D = F // HEADS[l]
                    with pe.Fori(0, T // 2) as i:
                        for b in range(2):
                            n = inst * T + 2 * i + b
                            pe.wait_ge(x_diag, n + 1)
                            nc.tensor.matmul(psX[b][:, 0:P], ONE[:], X_DIAG[:, b, :], start=True, stop=True
                                             ).then_inc(x_tb, 1)
                            pe.wait_ge(x_tbc, n + 1)
                    with pe.Fori(0, T) as t:
                        no = inst * T + t
                        pe.wait_ge(x_pr, no + 1)
                        nc.tensor.matmul(psM[1][:, 0:D], ZERO[:], ZERO[:, 0:D], start=True, stop=False,
                                         skip_group_check=True)
                        with pe.Fori(0, T // 8) as g:
                            for b in range(2):
                                pe.wait_ge(x_stg, no * (T // 4) + 2 * g + b + 1)
                                for c in range(4):
                                    tr = nc.tensor.transpose(psX[b][:, c * P:(c + 1) * P],
                                                             X_ST[:, b, c * P:(c + 1) * P], IDN[:])
                                tr.then_inc(x_tr, 1)
                                pe.wait_ge(x_trc, no * (T // 4) + 2 * g + b + 1)
                                for c in range(4):
                                    nc.tensor.matmul(psM[1][:, 0:D], X_PT[:, b, c * P:(c + 1) * P],
                                                     TBL[:, 8 * g + 4 * b + c, h * D:(h + 1) * D],
                                                     start=False, stop=False, skip_group_check=True)
                        nc.tensor.matmul(psM[1][:, 0:D], ZERO[:], ZERO[:, 0:D], start=False, stop=True,
                                         skip_group_check=True).then_inc(x_acc, 1)
                    if h == HEADS[l] - 1 and l < 3:
                        project_quad(l + 1, 0)
                        average_quad(l + 1, 0)
                        with pe.Fori(1, QUADS - 1) as q:
                            project_quad(l + 1, q)
                            average_quad(l + 1, q)
                        project_quad(l + 1, QUADS - 1)
                        average_quad(l + 1, QUADS - 1)

        @block.scalar
        def _(act):
            a = nc.scalar
            for l in range(4):
                act.wait_ge(wt_made, l + 1)
                a.activation(WT[:], psT[0][:, 0:P], ACT.Copy).then_inc(wt_copied, 1)
                act.wait_ge(wa_made, l + 1)
                a.activation(WA[:, l, F:TW], psW[0][:, 0:8], ACT.Copy).then_inc(wa_copied, 1)

            def centre(rows, moments, j):
                act.wait_ge(moments_made, moments)
                a.activation(HN[:, j, :], rows, ACT.Identity, bias=NM[:, j:j + 1]).then_inc(hn_made, 1)

            def rectify(no, j):
                act.wait_ge(ht_psum, no + 1)
                a.activation(HT[:, j % 2, :], psT[j % 2][:, 0:P], ACT.Relu).then_inc(ht_made, 1)

            def keep_raw(t, j):
                act.wait_ge(wh_made, t + 1)
                a.activation(TBL[:, t, :], psW[j][:, 0:TW], ACT.Copy).then_inc(raw_kept, 1)

            def centre_quad(l, q):
                for j in range(4):
                    centre(REC[:, 4 * q + j, 0:F], T + QUADS * l + q + 1, j)

            def rectify_quad(l, q):
                for j in range(4):
                    rectify(T * (l + 1) + 4 * q + j, j)

            def keep_quad(l, q):
                act.wait_ge(rstd_made, 2 + QUADS * l + q)
                for j in range(4):
                    t = 4 * q + j
                    act.wait_ge(wh_made, T * (l + 1) + t + 1)
                    a.activation(TBL[:, t, :], psW[j][:, 0:TW], ACT.Copy, scale=RSTD[:, bass.ds(t, 1)]
                                 ).then_inc(tb_made, 1)

            act.wait_ge(consts, 1)

            def make_mask(i, h):
                act.wait_ge(adj_loaded[h % 4], 32 * i + 16 * (h // 4) + 16)
                if not (type(i) is int and h < 2):
                    act.wait_ge(mask_read, 8 * i + h - 1)
                a.activation(mask[:, h % 2, :], AREA[:, h % 4, :], ACT.Sigmoid, bias=C100[:], scale=200.0,
                             accum_out=DEGH[:, bass.ds(8 * i + h, 1)]).then_inc(mask_made, 1)

            def extract_quad(i):
                first = type(i) is int
                for j in range(4):
                    t = 4 * i + j
                    make_mask(i, 2 * j)
                    if not (first and j < 2):
                        keep_raw(t - 2, (j - 2) % 4)
                    if not (first and j < 1):
                        centre(REC[:, t - 1, 0:F], t, (j - 1) % 4)
                    make_mask(i, 2 * j + 1)
                    if not (first and j < 1):
                        rectify(t - 1, (j - 1) % 4)

            extract_quad(0)
            with act.Fori(1, QUADS) as i:
                extract_quad(i)
            keep_raw(T - 2, 2)
            centre(REC[:, T - 1, 0:F], T, 3)
            rectify(T - 1, 3)
            keep_raw(T - 1, 3)
            act.drain()
            act.wait_ge(rstd_made, 1)
            with act.Fori(0, T) as t:
                a.activation(TBL[:, t, :], TBL[:, t, :], ACT.Copy, scale=RSTD[:, bass.ds(t, 1)]).then_inc(tb_made, 1)

            def exp_scores(l, q, k):
                n = 4 * k * HEADS[l]
                act.wait_ge(sc_made, QUADS * l + q + 1)
                a.activation(PRB[:, 0:n], SCO[:, 0:n], ACT.Exp).then_inc(exp_made, 1)

            def exp_negative(l, q):
                act.wait_ge(h_made, QUADS * l + q + 1)
                a.activation(NEG, HH, ACT.Relu, scale=-1.0)
                act.drain()
                a.activation(EX[:], NEG, ACT.Exp, scale=-1.0).then_inc(ex_made, 1)

            act.wait_ge(flag_ready, 1)
            overflow = act.value_load(FLAGI[0:1, 0:1])
            with act.If(overflow == 0):
                for l in range(4):
                    def quad(q):
                        exp_negative(l, q)
                        if l < 3:
                            centre_quad(l, q)
                            rectify_quad(l, q)
                        if not (type(q) is int and q == QUADS - 1):
                            exp_scores(l, q + 1, QMAX)
                        if l < 3:
                            keep_quad(l, q)

                    exp_scores(l, 0, SLOTS)
                    quad(0)
                    with act.Fori(1, QUADS - 1) as q:
                        quad(q)
                    quad(QUADS - 1)
            with act.Else():
                for inst, (l, h) in enumerate(INST):
                    D = F // HEADS[l]
                    with act.Fori(0, T // 2) as i:
                        for b in range(2):
                            act.wait_ge(x_tb, inst * T + 2 * i + b + 2)
                            nc.scalar.activation(X_T[:, bass.ds(i * (2 * P) + b * P, P)], psX[b][:, 0:P], ACT.Copy
                                                 ).then_inc(x_tbc, 1)
                    with act.Fori(0, T) as t:
                        no = inst * T + t
                        act.wait_ge(x_sc, no + 1)
                        nc.scalar.activation(X_E, X_E, ACT.Exp, bias=X_M[:, 1:2], accum_out=X_M[:, 2:3]
                                             ).then_inc(x_exp, 1)
                        with act.Fori(0, T // 8) as g:
                            for b in range(2):
                                act.wait_ge(x_tr, no * (T // 4) + 2 * g + b + 2)
                                nc.scalar.activation(X_PT[:, b, :], psX[b][:], ACT.Copy).then_inc(x_trc, 1)
                        act.wait_ge(x_en, no + 1)
                        nc.scalar.activation(X_E1[:, 0:D], X_H[:, 0:D], ACT.Exp).then_inc(x_ex, 1)
                    if h == HEADS[l] - 1 and l < 3:
                        with act.Fori(0, QUADS) as q:
                            centre_quad(l, q)
                            rectify_quad(l, q)
                            keep_quad(l, q)

        def moments(dve, v, q):
            for j in range(4):
                v.bn_stats(ST[:, j, :], REC[:, 4 * q + j, 0:F])
            dve.drain()
            for j in range(4):
                v.bn_aggr(MV[:, j, :], ST[:, j, :])
            dve.drain()
            v.tensor_scalar(NM[:], MV[:, :, 0], -1.0, None, ALU.mult).then_inc(moments_made, 1)
            v.tensor_scalar(VAR[:, bass.ds(4 * q, 4)], MV[:, :, 1], EPS, None, ALU.add)

        def seed_bits(v, t, n, step):
            at = bass.ds(t, n)
            if step == 0:
                v.tensor_scalar(SEED[:, 0:n], VAR[:, at].bitcast(I32), 1, None, ALU.arith_shift_right)
            else:
                v.tensor_scalar(RSTD[:, at].bitcast(I32), SEED[:, 0:n], -1.0, float(0x5F3759DF),
                                ALU.mult, ALU.add)

        def newton(v, t, n, step):
            at = bass.ds(t, n)
            y, u = RSTD[:, at], NEWT[:, 0:n]
            if step == 0:
                return v.tensor_tensor(u, y, y, ALU.mult)
            if step == 1:
                return v.scalar_tensor_tensor(u, u, -0.5, VAR[:, at], ALU.mult, ALU.mult)
            return v.scalar_tensor_tensor(y, u, 1.5, y, ALU.add, ALU.mult)

        def deviations(dve, v, t, n):
            dve.drain()
            for step in range(2):
                seed_bits(v, t, n, step)
                dve.drain()
            for step in range(9):
                last = newton(v, t, n, step % 3)
                if step < 8:
                    dve.drain()
            last.then_inc(rstd_made, 1)

        def fast(dve, v):
            v.memset(area[:, 0:8704 + 8 * QMAX * TW].bitcast(F32), 0.0)

            def read_lists(t, n):
                at = bass.ds(t, n)
                NL = REC[:, at, R_NL:R_NL + SLOTS]
                pads = PRV(n)
                v.tensor_scalar(VB[:, at, :], NL, 0.0, -BIG, ALU.is_equal, ALU.mult)
                v.tensor_scalar(pads, NL, 0.0, 8.0 * N, ALU.is_equal, ALU.mult)
                v.tensor_copy(IDU[:, at], REC[:, at, R_ID])
                dve.drain()
                v.memset(VB[:, at, 0:1], 0.0)
                v.tensor_scalar(pads[:, :, 0:1], pads[:, :, 0:1], (N + 1) / (8.0 * N), None, ALU.mult)
                dve.drain()
                v.scalar_tensor_tensor(NLU[:, at, :], NL, -1.0, pads, ALU.add, ALU.add)
                dve.drain()

            def PRV(n):
                return PR[:, 0:n * SLOTS].rearrange("p (t s) -> p t s", s=SLOTS)

            dve.wait_ge(rec_loaded, 16)
            read_lists(0, 4)
            dve.wait_ge(rec_loaded, 32)
            read_lists(4, T - 4)
            v.memset(MX[:, 0:1], 0.0).then_inc(lists_ready, 1)

            for l in range(4):
                if l > 0:
                    mean_row(dve, v, l)
                scores(dve, v, l, 0, None, SLOTS)
                attend(dve, v, l, 0, SLOTS, SLOTS, G0)
                update(dve, v, l, 0)
                scores(dve, v, l, 1, 0, QMAX)
                for first, pairs, k in PAIR_RUNS:
                    for q in over(dve, first, pairs):
                        for b in range(2):
                            attend(dve, v, l, q + b, k, QMAX, GQ[b])
                            update(dve, v, l, q + b)
                            scores(dve, v, l, q + b + 1, q + b, QMAX, 1 - b,
                                   (first + b + 1, first + b + 3) if pairs > 1 else None)
                attend(dve, v, l, QUADS - 1, slots_of(QUADS - 1, 0), QMAX, GQ[0])
                update(dve, v, l, QUADS - 1)
                if l < 3:
                    deviations(dve, v, T - 4, 4)

        def over(eng, first, pairs):
            if pairs == 1:
                yield first
            else:
                with eng.Fori(first, first + 2 * pairs, 2) as q:
                    yield q

        def mean_row(dve, v, l):
            dve.wait_ge(mean_made, T * (l + 1))
            v.tensor_copy(MEANR[:, 0:F], psM[l % 2][0:1, 0:F])
            v.memset(MEANR[:, T_AUX:T_AUX + 1], 0.0).then_inc(meanrow_made, 1)

        def scores(dve, v, l, q, prev, k, b=0, run=None):
            H = HEADS[l]
            n = 4 * k * H
            g = G0 if k == SLOTS else GQ[b]
            tiles = bass.ds(4 * q, 4)
            sco = SCO[:, 0:n].rearrange("p (j s h) -> p j s h", j=4, h=H)
            per_slot = lambda ap: ap.unsqueeze(2).to_broadcast([P, 4, k, H])
            heads = lambda ap: ap[:, 0:4 * H].rearrange("p (j h) -> p j h", j=4)
            aux1 = AUX1[:, 0:4 * k].rearrange("p (j s) -> p j s", j=4)
            at = None if prev is None or l == 3 else 4 * prev
            src = REC[:, tiles, R_S:R_S + H] if l == 0 else TBL[:, tiles, T_S:T_S + H]

            if l > 0 and k == SLOTS:
                dve.wait_ge(tb_made, T * (l + 1))
            if k == SLOTS:
                dve.wait_ge(gathered[0], landed_by(0) * (l + 1))
            else:
                of_layer = landed_by(QUADS - 1 - b)
                if type(q) is int:
                    dve.wait_ge(gathered[1 + b], l * of_layer + landed_by(q))
                else:
                    start, end = run
                    step = (landed_by(end) - landed_by(start)) // (end - start)
                    dve.wait_ge(gathered[1 + b], q * step + (l * of_layer + landed_by(start) - step * start))
            v.tensor_tensor(sco, g[:, :, 0:k, T_T:T_T + H], per_slot(src), ALU.add)
            if l == 1:
                v.tensor_scalar(aux1, g[:, :, 0:k, T_AUX], 0.0, 1.0, ALU.not_equal, ALU.subtract)
            if at is not None:
                seed_bits(v, at, 4, 0)
            dve.drain()
            v.scalar_tensor_tensor(SCO[:, 0:n], SCO[:, 0:n], ALPHA, SCO[:, 0:n], ALU.mult, ALU.max)
            if l == 1:
                v.scalar_tensor_tensor(aux1, aux1, BIG, VB[:, tiles, 0:k], ALU.mult, ALU.add)
            if at is not None:
                seed_bits(v, at, 4, 1)
            dve.drain()
            if l == 1:
                v.tensor_tensor(SCO[:, 0:n], SCO[:, 0:n], AUX1[:, 0:n], ALU.add)
                v.tensor_scalar(AUX2[:, 0:n], AUX1[:, 0:n], 0.0, None, ALU.is_equal)
            else:
                v.tensor_tensor(sco, sco, VB[:, tiles, 0:k].unsqueeze(3).to_broadcast([P, 4, k, H]), ALU.add)
            if at is not None:
                newton(v, at, 4, 0)
            dve.drain()
            v.tensor_reduce(heads(MX), sco.rearrange("p j s h -> p j h s"), AX.X, ALU.max)
            if l == 1:
                v.tensor_reduce(LCNT, AUX2[:, 0:n].rearrange("p (j s) -> p j s", j=4), AX.X, ALU.add)
            if at is not None:
                newton(v, at, 4, 1)
            dve.drain()
            if l == 1:
                v.tensor_scalar(MX[:, 0:4], MX[:, 0:4], FLOOR, None, ALU.max)
                dve.drain()
            v.tensor_tensor(sco, sco, per_slot(heads(MX)), ALU.subtract).then_inc(sc_made, 1)
            if at is not None:
                last = newton(v, at, 4, 2)
                for step in range(3, 9):
                    dve.drain()
                    last = newton(v, at, 4, step % 3)
                last.then_inc(rstd_made, 1)

        def attend(dve, v, l, q, k, kk, g):
            H = HEADS[l]
            n = 4 * kk * H
            tiles = bass.ds(4 * q, 4)
            prb = PRB[:, 0:n].rearrange("p (j s h) -> p j s h", j=4, h=H)
            per_slot = lambda ap: ap.unsqueeze(2).to_broadcast([P, 4, kk, H])
            heads = lambda ap: ap[:, 0:4 * H].rearrange("p (j h) -> p j h", j=4)
            pr = PR[:, 0:4 * k * F].rearrange("p (j s f) -> p j s f", j=4, f=F)
            dve.wait_ge(exp_made, QUADS * l + q + 1)
            v.tensor_reduce(heads(Z), prb.rearrange("p j s h -> p j h s"), AX.X, ALU.add)
            dve.drain()
            if l == 1:
                v.tensor_scalar(Z[:, 0:4], Z[:, 0:4], 1e-30, None, ALU.max)
                dve.drain()
            v.reciprocal(RZ[:, 0:4 * H], Z[:, 0:4 * H])
            dve.drain()
            v.tensor_tensor(prb, prb, per_slot(heads(RZ)), ALU.mult)
            dve.drain()
            if l == 1:
                v.tensor_reduce(TOPA, prb[:, :, :, 0], AX.X, ALU.max)
                v.scalar_tensor_tensor(AUX1[:, 0:n], PRB[:, 0:n], THR, PRB[:, 0:n], ALU.is_ge, ALU.mult)
                dve.drain()
                v.scalar_tensor_tensor(RZ[:, 0:4], TOPA, THR, LCNT, ALU.is_gt, ALU.mult)
                dve.drain()
                v.tensor_tensor(prb[:, :, :, 0], AUX1[:, 0:n].rearrange("p (j s) -> p j s", j=4),
                                RZ[:, 0:4].unsqueeze(2).to_broadcast([P, 4, kk]), ALU.mult)
                dve.drain()
            if H == 1:
                used = v.tensor_tensor(pr, g[:, :, 0:k, 0:F], prb[:, :, 0:k, :].to_broadcast([P, 4, k, F]), ALU.mult)
            else:
                for j in range(4):
                    used = v.tensor_tensor(pr[:, j].rearrange("p s (h d) -> p s h d", h=H),
                                    g[:, j, 0:k, 0:F].rearrange("p s (h d) -> p s h d", h=H),
                                    prb[:, j, 0:k, :].unsqueeze(3).to_broadcast([P, k, H, F // H]), ALU.mult)
            if l == 0:
                used = v.scalar_tensor_tensor(NLU[:, tiles, 0:k], VB[:, tiles, 0:k], -8.0 * N / BIG, g[:, :, 0:k, T_AUX],
                                       ALU.mult, ALU.add)
            elif l < 3:
                used = v.tensor_scalar(NLU[:, tiles, :], NLU[:, tiles, :], float(NT if l == 2 else -NT), None, ALU.add)
            used.then_inc(g_free, 1)
            dve.drain()
            summed = v.tensor_reduce(HH, pr.rearrange("p j s f -> p j f s"), AX.X, ALU.add)
            if l == 1:
                dve.drain()
                summed = v.tensor_tensor(HH, HH, TBL[:, tiles, 0:F], ALU.add)
            summed.then_inc(h_made, 1)

        def update(dve, v, l, q):
            rows = REC[:, bass.ds(4 * q, 4), 0:F]
            dve.drain()
            v.scalar_tensor_tensor(POS, HH, 0.0, rows, ALU.max, ALU.add)
            dve.drain()
            dve.wait_ge(ex_made, QUADS * l + q + 1)
            if l == 3:
                v.scalar_tensor_tensor(rows, EX[:], -1.0, POS, ALU.add, ALU.add).then_inc(x_final, 1)
            else:
                v.scalar_tensor_tensor(rows, EX[:], -1.0, POS, ALU.add, ALU.add)
                dve.drain()
                moments(dve, v, q)
                dve.drain()

        def dense(dve, v):
            for inst, (l, h) in enumerate(INST):
                D = F // HEADS[l]
                if h == 0:
                    dve.wait_ge(mean_made, T * (l + 1))
                    v.tensor_copy(MEAN[:], psM[l % 2][:, 0:F])
                v.tensor_copy(X_TC, TBL[:, :, T_T + h])
                if l == 1:
                    v.tensor_scalar(X_TG, TBL[:, :, T_AUX], 0.0, 1.0, ALU.not_equal, ALU.subtract)
                    dve.drain()
                    v.scalar_tensor_tensor(X_TC, X_TG, BIG, X_TC, ALU.mult, ALU.add)
                dve.drain()
                with dve.Fori(0, T // 2) as i:
                    for b in range(2):
                        dve.wait_ge(x_tb, inst * T + 2 * i + b + 1)
                        v.tensor_scalar(X_DIAG[:, b, :], IDN[:], X_TC[:, bass.ds(2 * i + b, 1)], None, ALU.mult
                                        ).then_inc(x_diag, 1)
                dve.wait_ge(x_tbc, (inst + 1) * T)
                with dve.Fori(0, T) as t:
                    no = inst * T + t
                    v.memset(X_M[:, 3:4], 0.0).then_inc(x_adj_free, 1)
                    dve.wait_ge(x_adj, 16 * no + 16)
                    v.tensor_scalar(X_BIAS, X_ADJ, 0.0, 1.0, ALU.is_gt, ALU.subtract)
                    v.tensor_scalar(X_E, X_T, TBL[:, t, T_S + h:T_S + h + 1], None, ALU.add)
                    dve.drain()
                    v.scalar_tensor_tensor(X_E, X_E, ALPHA, X_E, ALU.mult, ALU.max)
                    dve.drain()
                    v.scalar_tensor_tensor(X_E, X_BIAS, BIG, X_E, ALU.mult, ALU.add)
                    dve.drain()
                    v.tensor_reduce(X_M[:, 0:1], X_E, AX.X, ALU.max)
                    if l == 1:
                        v.tensor_scalar(X_BIAS, X_E, FLOOR, None, ALU.is_gt)
                        dve.drain()
                        v.tensor_reduce(X_M[:, 3:4], X_BIAS, AX.X, ALU.add)
                    dve.drain()
                    v.tensor_scalar(X_M[:, 1:2], X_M[:, 0:1], FLOOR, -1.0, ALU.max, ALU.mult).then_inc(x_sc, 1)
                    dve.wait_ge(x_exp, no + 1)
                    v.tensor_scalar(X_M[:, 4:5], X_M[:, 2:3], 1e-30, None, ALU.max)
                    v.tensor_scalar(X_M[:, 6:7], X_M[:, 2:3], 0.0, None, ALU.is_equal)
                    dve.drain()
                    v.reciprocal(X_M[:, 5:6], X_M[:, 4:5])
                    dve.drain()
                    if l == 1:
                        v.tensor_scalar(X_E, X_E, X_M[:, 5:6], None, ALU.mult)
                        dve.drain()
                        v.tensor_reduce(X_M[:, 7:8], X_E, AX.X, ALU.max)
                        v.scalar_tensor_tensor(X_E, X_E, THR, X_E, ALU.is_ge, ALU.mult)
                        dve.drain()
                        v.scalar_tensor_tensor(X_M[:, 5:6], X_M[:, 7:8], THR, X_M[:, 3:4], ALU.is_gt, ALU.mult)
                        dve.drain()
                        v.tensor_copy(X_H[:, 0:D], TBL[:, t, 0:D]).then_inc(x_pr, 1)
                    else:
                        v.tensor_scalar(X_H[:, 0:D], MEAN[:, h * D:(h + 1) * D], X_M[:, 6:7], None, ALU.mult
                                        ).then_inc(x_pr, 1)
                    dve.drain()
                    with dve.Fori(0, T // 8) as g:
                        for b in range(2):
                            dve.wait_ge(x_tr, no * (T // 4) + 2 * g + b + 1)
                            v.tensor_copy(X_ST[:, b, :], X_E[:, bass.ds(g * (8 * P) + b * (4 * P), 4 * P)]
                                          ).then_inc(x_stg, 1)
                    dve.wait_ge(x_acc, no + 1)
                    v.scalar_tensor_tensor(X_H[:, 0:D], psM[1][:, 0:D], X_M[:, 5:6], X_H[:, 0:D], ALU.mult, ALU.add)
                    dve.drain()
                    x_rows = REC[:, t, h * D:(h + 1) * D]
                    v.scalar_tensor_tensor(x_rows, X_H[:, 0:D], 0.0, x_rows, ALU.max, ALU.add)
                    v.tensor_scalar(X_H[:, 0:D], X_H[:, 0:D], 0.0, None, ALU.min).then_inc(x_en, 1)
                    dve.drain()
                    dve.wait_ge(x_ex, no + 1)
                    v.scalar_tensor_tensor(x_rows, X_E1[:, 0:D], -1.0, x_rows, ALU.add, ALU.add)
                    dve.drain()
                if h == HEADS[l] - 1 and l < 3:
                    with dve.Fori(0, QUADS) as q:
                        moments(dve, v, q)
                        deviations(dve, v, 4 * q, 4)
            v.memset(X_M[:, 0:1], 0.0).then_inc(x_out, 1)

        @block.vector
        def _(dve):
            v = nc.vector
            v.memset(AV[:], 0.0)
            dve.drain()
            v.memset(AV[:, 1, 1:2], 1.0).then_inc(av_set, 1)
            v.memset(ONEN[:], 1.0 / N)
            v.memset(ZERO[:], 0.0)
            v.memset(MEANR[:], 0.0)
            v.memset(C100[:], -100.0).then_inc(consts, 1)
            dve.wait_ge(x_loaded, 16)
            dve.wait_ge(iotas, 5)
            v.tensor_copy(REC[:, :, R_ID], RANKU[:])
            v.memset(REC[:, :, R_ID + 1:RW], 0.0).then_inc(lists_free, 1)

            def codes_of(i, j, half):
                dve.wait_ge(mask_made, 8 * i + 2 * j + half + 1)
                v.tensor_tensor(code[:, half, :], mask[:, half, :].bitcast(U16),
                                pair_code[:, half * HP:(half + 1) * HP], ALU.mult).then_inc(mask_read, 1)

            def candidates(j, half):
                for s in range(SEGS):
                    at = (half * SEGS + s) * 8
                    v.max(CND[:, j % 2, at:at + 8], code[:, half, s * SEG:(s + 1) * SEG])

            def hand_codes(j, first):
                op = v.tensor_copy(CQ[:, j, :], TOP[:, j, :])
                if j == 3:
                    op.then_inc(codes_ready, 1)

            def lists_largest(n):
                dve.wait_ge(decoded, n)
                dve.nop(nofuse=True)
                for j in range(4):
                    v.max(S16[:, j, 0:8], L32[:, j, :])

            def lists_replace():
                for j in range(4):
                    op = v.match_replace(S32[:, j, :], S16[:, j, 0:8], L32[:, j, :], 0.0)
                op.then_inc(lists_free, 1)

            def lists_next():
                for j in range(4):
                    v.max(S16[:, j, 8:16], S32[:, j, :])

            def extract_quad(i):
                first = type(i) is int
                for j in range(4):
                    t = 4 * i + j
                    p1, p2 = (j - 1) % 4, (j - 2) % 4
                    codes_of(i, j, 0)
                    v.bn_stats(ST[:, j, :], REC[:, t, 0:F])
                    dve.drain()
                    candidates(j, 0)
                    if not (first and j < 1):
                        v.max(TOP[:, p1, 0:8], CND[:, p1 % 2, :])
                    if not (first and j < 2):
                        v.max(TOP[:, p2, 8:16], CND2)
                    v.bn_aggr(MV[:, j, :], ST[:, j, :])
                    if not first and j == 3:
                        lists_replace()
                    codes_of(i, j, 1)
                    dve.drain()
                    candidates(j, 1)
                    if not (first and j < 1):
                        v.match_replace(CND2, TOP[:, p1, 0:8], CND[:, p1 % 2, :], 0.0)
                    v.tensor_scalar(NM[:, j:j + 1], MV[:, j, 0:1], -1.0, None, ALU.mult).then_inc(moments_made, 1)
                    v.tensor_scalar(VAR[:, bass.ds(t, 1)], MV[:, j, 1:2], EPS, None, ALU.add)
                    if not first and j == 2:
                        dve.wait_ge(codes_taken, i)
                    if not (first and j < 2):
                        hand_codes(p2, first)
                    if not first and j == 2:
                        lists_largest(i)
                    if not first and j == 3:
                        lists_next()
                        dve.drain()
                        v.tensor_copy(REC[:, bass.ds(4 * i - 4, 4), R_NL:R_NL + SLOTS], S16)

            extract_quad(0)
            with dve.Fori(1, QUADS) as i:
                extract_quad(i)
            dve.drain()
            v.max(TOP[:, 3, 0:8], CND[:, 1, :])
            v.max(TOP[:, 2, 8:16], CND2)
            dve.drain()
            v.match_replace(CND2, TOP[:, 3, 0:8], CND[:, 1, :], 0.0)
            hand_codes(2, False)
            dve.drain()
            v.max(TOP[:, 3, 8:16], CND2)
            dve.drain()
            hand_codes(3, False)
            deviations(dve, v, 0, T)

            v.tensor_tensor(DEG[:], DEGH[:, 0:2 * T:2], DEGH[:, 1:2 * T:2], ALU.add)
            for k in range(NC):
                v.memset(CLS[:, k, :], float(SLOTS - k))
            v.memset(ONEB, 1.0)
            dve.wait_ge(upper_made, 1)
            v.tensor_copy(UPPER, UPPERF)
            dve.drain()
            v.tensor_scalar(DEG[:], DEG[:], ROUND, None, ALU.add)
            dve.drain()
            v.tensor_scalar(DEG[:], DEG[:], ROUND, None, ALU.subtract)
            dve.drain()
            v.tensor_scalar(DCAP, DEG[:], float(SLOTS), None, ALU.min)
            dve.drain()
            v.tensor_tensor(OHB, CLS, DCAP.unsqueeze(1).to_broadcast([P, NC, T]), ALU.is_equal
                            ).then_inc(onehot_made, 1)
            lists_largest(QUADS)
            dve.drain()
            lists_replace()
            dve.drain()
            lists_next()
            dve.drain()
            v.tensor_copy(REC[:, T - 4:T, R_NL:R_NL + SLOTS], S16)
            dve.drain()
            v.tensor_scalar(VALID, REC[:, :, R_NL:R_NL + SLOTS], 0.0, None, ALU.is_gt)

            def bank(i):
                return i * 512, min(512, NC * T - i * 512)

            tot = TOT.rearrange("p c t -> p (c t)")
            dve.wait_ge(prefix_made, 3)
            for i, src in enumerate((psX[0], psX[1], psW[1])):
                at, w = bank(i)
                v.tensor_copy(tot[:, at:at + w], src[:, 0:w])
            dve.drain()
            v.tensor_reduce(CNT, VALID, AX.X, ALU.add)
            src, step, n = TOT, 1, 0
            while step < T:
                dst = SC[n % 2]
                v.tensor_tensor(dst[:, :, step:], src[:, :, step:], src[:, :, :T - step], ALU.add)
                v.tensor_copy(dst[:, :, 0:step], src[:, :, 0:step])
                dve.drain()
                if n == 0:
                    v.tensor_tensor(MIS, CNT, DEG[:], ALU.not_equal)
                if n == 1:
                    v.tensor_reduce(FLAG[:, 0:1], MIS, AX.X, ALU.add)
                src, step, n = dst, 2 * step, n + 1
            run_t, other = src, SC[n % 2]
            v.memset(CT[0][:, 0:1], 0.0)
            v.tensor_copy(CT[0][:, 1:NC + 1], run_t[:, :, T - 1])
            v.tensor_tensor(other, run_t, TOT, ALU.subtract)
            dve.drain()
            m, step = 0, 1
            while step < NC + 1:
                v.tensor_tensor(CT[1 - m][:, step:], CT[m][:, step:], CT[m][:, :NC + 1 - step], ALU.add)
                v.tensor_copy(CT[1 - m][:, 0:step], CT[m][:, 0:step])
                dve.drain()
                m, step = 1 - m, 2 * step
            above = CT[m]
            v.tensor_tensor(other, other, above[:, 0:NC].unsqueeze(2).to_broadcast([P, NC, T]), ALU.add)
            dve.drain()
            flat = other.rearrange("p c t -> p (c t)")
            dve.wait_ge(prefix_made, 6)
            for i, src in enumerate((psT[0], psT[1], psW[0])):
                at, w = bank(i)
                v.tensor_tensor(flat[:, at:at + w], flat[:, at:at + w], src[:, 0:w], ALU.add)
            dve.drain()
            v.tensor_tensor(other, other, OHB, ALU.mult)
            dve.drain()
            v.tensor_reduce(RANKF[:], other.rearrange("p c t -> p t c"), AX.X, ALU.add)
            for quad in range(QUADS):
                for j in range(4 if quad == 0 else 1):
                    k = slots_of(quad, j)
                    if k < SLOTS and not (quad > 1 and QUAD_SLOTS[quad - 2] == k):
                        v.scalar_tensor_tensor(FLAG[:, 0:1], above[:, SLOTS - k:SLOTS - k + 1],
                                               P * (4 * quad + j) + 0.5, FLAG[:, 0:1], ALU.is_gt, ALU.add)
                        dve.drain()
            v.tensor_copy(RANKU[:], RANKF[:])
            v.tensor_copy(FLAG[:, 1:2], FLAG[:, 0:1]).then_inc(miss_made, 1)
            dve.wait_ge(tb_made, T)
            v.tensor_scalar(TBL[:, :, T_AUX], RANKF[:], float(NT), None, ALU.add)
            v.tensor_copy(REC[:, :, R_S:R_S + 4], TBL[:, :, T_S:T_S + 4]).then_inc(rank_ready, 1)
            dve.wait_ge(flag_summed, 1)
            v.tensor_copy(FLAGI[:], psM[1][:, 0:1]).then_inc(flag_ready, 1)
            v.tensor_copy(MEANR[:, 0:F], psM[0][0:1, 0:F])
            v.memset(MEANR[:, T_AUX:T_AUX + 1], float(N + NT)).then_inc(meanrow_made, 1)
            dve.wait_ge(flag_ready, 1)
            overflow = dve.value_load(FLAGI[0:1, 0:1])
            with dve.If(overflow == 0):
                fast(dve, v)
            with dve.Else():
                dense(dve, v)


_INS = ["x", "adj", "L0_gnn_W", "L0_gnn_a", "L1_gnn_W", "L1_gnn_a", "L2_gnn_W", "L2_gnn_a",
        "L3_gnn_W", "L3_gnn_a"]
_OUTS = [((8192, 128), "float32")]


def kernel(**inputs):
    import numpy as _np
    import concourse.bacc as _bacc
    from concourse import mybir as _mybir
    from concourse.bass_utils import run_bass_kernel_spmd as _run

    nc = _bacc.Bacc("TRN2", target_bir_lowering=False, num_devices=1)
    arrays, args = {}, []
    for name in _INS:
        a = _np.ascontiguousarray(inputs[name])
        arrays[f"in_{name}_dram"] = a
        args.append(nc.dram_tensor(f"in_{name}_dram", a.shape, _mybir.dt.from_np(a.dtype), kind="ExternalInput").ap())
    for i, (shape, dtype) in enumerate(_OUTS):
        dt = _mybir.dt.from_np(_np.dtype(dtype))
        args.append(nc.dram_tensor(f"out_{i}_dram", shape, dt, kind="ExternalOutput").ap())
    gat_kernel(nc, *args)
    r = _run(nc, [arrays], core_ids=[0])
    return r.results[0]["out_0_dram"]
```

```python
from contextlib import ExitStack

import concourse.bass as bass
from concourse import mybir

ALU = mybir.AluOpType
ACT = mybir.ActivationFunctionType
AX = mybir.AxisListType
F32 = mybir.dt.float32
BF16 = mybir.dt.bfloat16
U8 = mybir.dt.uint8
U16 = mybir.dt.uint16
U32 = mybir.dt.uint32
I32 = mybir.dt.int32

P = 128
EPS = 1e-5
ALPHA = 0.2
THR = 1e-4
BIG = 2.0 ** 100
FLOOR = -2.0 ** 90
ROUND = 12582912.0
SLOTS = 16
HEADS = [1, 1, 4, 1]

BY_DEGREE = [16, 9, 8, 8] + [7] * 4 + [6] * 7 + [5] * 10 + [4] * 13 + [3] * 12 + [2] * 9 + [1] * 5
BIG_QUAD = 3
FIRST_RING = 4
FIRST_LAST = 13
PAIR_RUNS = [(4, 7), (8, 5)]
AFTER_RUNS = 12

R_S, R_NL, R_ID, RW = 128, 132, 148, 152
T_T, T_AUX, T_S, TW = 128, 129, 132, 136


def slots_of(quad, j):
    return BY_DEGREE[(4 * (quad - BIG_QUAD) + j) % len(BY_DEGREE)]


SMALL_MAX = slots_of(0, 0)
QMAX = slots_of(FIRST_RING, 0)
LAST_MAX = slots_of(FIRST_LAST, 0)


def score_slots(quad):
    if quad < BIG_QUAD:
        return SMALL_MAX
    if quad == BIG_QUAD:
        return SLOTS
    return QMAX if quad < FIRST_LAST else LAST_MAX


def gat_kernel(nc, x, adj, W0, a0, W1, a1, W2, a2, W3, a3, out):
    N, F = x.shape
    T = N // P
    QUADS = T // 4
    SMALL_TILES = 4 * BIG_QUAD
    SHIFT = P * SMALL_TILES
    HALF = N // 2
    HP = HALF // 2
    SEG = 512
    SEGS = HP // SEG
    CAND = 2 * SEGS * 8
    NC = SLOTS + 1
    NT = N + 1
    ODD0 = N + 1
    Ws, As = [W0, W1, W2, W3], [a0, a1, a2, a3]
    INST = [(l, h) for l in range(4) for h in range(HEADS[l])]

    rec_d = nc.dram_tensor("records_sorted", (N, RW), F32, kind="Internal").ap()
    tab_d = nc.dram_tensor("tables", (2 * NT, TW), F32, kind="Internal").ap()

    with ExitStack() as ctx:
        def sb(name, shape, dt):
            return ctx.enter_context(nc.sbuf_tensor(name, shape, dt))

        def sem(name):
            return ctx.enter_context(nc.semaphore(name))

        REC = sb("REC", [P, T, RW], F32)
        TBL = sb("TBL", [P, T, TW], F32)
        WA = sb("WA", [P, 4, TW], F32)
        WT = sb("WT", [P, P], F32)
        AV = sb("AV", [P, 4, 8], F32)
        IDN = sb("IDN", [P, P], F32)
        ONE = sb("ONE", [P, P], F32)
        ONEN = sb("ONEN", [P, P], F32)
        ZERO = sb("ZERO", [P, P], F32)
        MEAN = sb("MEAN", [P, F], F32)
        MEANR = sb("MEANR", [1, TW], F32)
        C100 = sb("C100", [P, 1], F32)
        ST = sb("ST", [P, 4, 6], F32)
        MV = sb("MV", [P, 4, 2], F32)
        NM = sb("NM", [P, 4], F32)
        VAR = sb("VAR", [P, T], F32)
        RSTD = sb("RSTD", [P, T], F32)
        NEWT = sb("NEWT", [P, 4], F32)
        SEED = sb("SEED", [P, 4], I32)
        HN = sb("HN", [P, 4, F], F32)
        HT = sb("HT", [P, 2, F], F32)
        NLU = sb("NLU", [P, T, SLOTS], U32)
        IDU = sb("IDU", [P, T], U32)
        DEGH = sb("DEGH", [P, 2 * T], F32)
        DEG = sb("DEG", [P, T], F32)
        RANKF = sb("RANKF", [P, T], F32)
        RANKU = sb("RANKU", [P, T], U32)
        FLAG = sb("FLAG", [P, 4], F32)
        FLAGI = sb("FLAGI", [P, 1], I32)

        AREA = sb("AREA", [P, 4, HALF], I32)
        AREB = sb("AREB", [P, 8192], F32)
        AREC = sb("AREC", [P, 3712], F32)
        area = AREA[:].rearrange("p a b -> p (a b)")

        def part(base, shape, dt=F32, of=None):
            n = 1
            for s in shape:
                n *= s
            of = area if of is None else of
            v = of[:, base:base + (n if dt in (F32, U32, I32) else n // 2)]
            if dt is not of.dtype:
                v = v.bitcast(dt)
            names = "abcd"[:len(shape)]
            if len(shape) == 1:
                return v
            return v.rearrange(f"p ({' '.join(names)}) -> p {' '.join(names)}",
                               **dict(zip(names, shape)))

        def part_c(base, shape, dt=F32):
            return part(base, shape, dt, AREC[:])

        mask = AREB[:, 0:2048].bitcast(U8).rearrange("p (b n) -> p b n", b=2)
        pair_code = AREB[:, 2048:4096].bitcast(U16)
        code = AREB[:, 4096:8192].rearrange("p (b n) -> p b n", b=2)
        CND = part_c(0, [2, CAND])
        CND2 = part_c(128, [CAND])
        TOP = part_c(192, [4, SLOTS])
        CQ = part_c(256, [4, SLOTS])
        D_R = part_c(320, [4, SLOTS])
        D_T = part_c(384, [4, SLOTS])
        D_ODD = part_c(448, [4, SLOTS])
        D_B = part_c(512, [4, SLOTS])
        D_W = part_c(576, [4, SLOTS])
        D_Q = part_c(640, [4, SLOTS])
        L32 = part_c(704, [4, 2 * SLOTS])
        S32 = part_c(832, [4, 2 * SLOTS])
        S16 = part_c(960, [4, SLOTS])
        LOWERF = part_c(1024, [P])

        CLS = part(0, [NC, T])
        OHB = part(2304, [NC, T], BF16)
        TOT = part(2944, [NC, T])
        SUMS = part(4096, [NC, T])
        FAULTS = part(6400, [NC])
        LOWER = part(6464, [P], BF16)
        ONEB = part(6528, [P], BF16)
        CNT = part(6592, [T])
        MIS = part(6656, [T])
        VALID = part(6720, [T, SLOTS])
        DCAP = part(7744, [T])

        RING_BASE = 4 * SLOTS * TW
        G_BIG = part(0, [4, SLOTS, TW])
        G_LAST = [part(b * 4 * LAST_MAX * TW, [4, LAST_MAX, TW]) for b in range(3)]
        G_RING = [part(RING_BASE + b * 4 * QMAX * TW, [4, QMAX, TW]) for b in range(2)]
        G_SMALL = [part(RING_BASE + 4 * QMAX * TW + b * 4 * SMALL_MAX * TW, [4, SMALL_MAX, TW])
                   for b in range(3)]

        def kind_of(quad):
            if quad < BIG_QUAD:
                return quad, G_SMALL[quad]
            if quad == BIG_QUAD:
                return 3, G_BIG
            if quad < FIRST_LAST:
                return 4 + quad % 2, G_RING[quad % 2]
            return quad - FIRST_LAST, G_LAST[quad - FIRST_LAST]
        PR = AREB[:]
        VB = part_c(0, [T, SLOTS])
        SCO = part_c(1024, [4 * SLOTS * 4])
        PRB = part_c(1280, [4 * SLOTS * 4])
        AUX1 = part_c(1536, [4 * SLOTS])
        AUX2 = part_c(1600, [4 * SLOTS])
        MX = part_c(1664, [16])
        Z = part_c(1680, [16])
        RZ = part_c(1696, [16])
        LCNT = part_c(1712, [4])
        COUNT = part_c(1716, [4])
        HH = part_c(1728, [4, F])
        POS = part_c(2240, [4, F])
        NEG = part_c(2752, [4, F])
        EX = sb("EX", [P, 4, F], F32)

        X_ADJ = part(0, [N], I32)
        X_BIAS = part(0, [N])
        X_E = part(N, [N])
        X_T = AREB[:, 0:N]
        X_TC = part_c(0, [T])
        X_TG = part_c(64, [T])
        X_DIAG = part_c(128, [2, P])
        X_ST = part_c(384, [2, 4 * P])
        X_PT = part_c(1408, [2, 4 * P])
        X_M = part_c(2432, [8])
        X_H = part_c(2440, [F])
        X_E1 = part_c(2568, [F])

        def ps(name):
            return ctx.enter_context(nc.psum_tensor(name, [P, 512], F32))

        psT = [ps("psT0"), ps("psT1")]
        psW = [ps("psW0"), ps("psW1"), ps("psX0"), ps("psX1")]
        psX = psW[2:]
        psM = [ps("psM0"), ps("psM1")]

        x_loaded = sem("x_loaded")
        w_loaded = sem("w_loaded")
        av_set = sem("av_set")
        consts = sem("consts")
        iotas = sem("iotas")
        wt_made = sem("wt_made")
        wt_copied = sem("wt_copied")
        wa_made = sem("wa_made")
        wa_copied = sem("wa_copied")
        adj_loaded = [sem(f"adj_loaded{b}") for b in range(4)]
        mask_made = sem("mask_made")
        mask_read = sem("mask_read")
        codes_ready = sem("codes_ready")
        codes_taken = sem("codes_taken")
        decoded = sem("decoded")
        lists_free = sem("lists_free")
        moments_made = sem("moments_made")
        hn_made = sem("hn_made")
        ht_psum = sem("ht_psum")
        ht_made = sem("ht_made")
        wh_made = sem("wh_made")
        raw_kept = sem("raw_kept")
        rstd_made = sem("rstd_made")
        tb_made = sem("tb_made")
        mean_made = sem("mean_made")
        meanrow_made = sem("meanrow_made")
        onehot_made = sem("onehot_made")
        prefix_made = sem("prefix_made")
        miss_made = sem("miss_made")
        flag_summed = sem("flag_summed")
        flag_ready = sem("flag_ready")
        rank_ready = sem("rank_ready")
        table_stored = sem("table_stored")
        rec_scattered = sem("rec_scattered")
        rec_loaded = sem("rec_loaded")
        lists_ready = sem("lists_ready")
        gathered = [sem(f"gathered_{k}") for k in ("own0", "own1", "own2", "big", "even", "odd")]
        g_free = sem("g_free")
        sc_made = sem("sc_made")
        exp_made = sem("exp_made")
        h_made = sem("h_made")
        ex_made = sem("ex_made")
        x_final = sem("x_final")
        out_stored = sem("out_stored")
        lower_made = sem("lower_made")
        x_adj = sem("dense_adj_loaded")
        x_adj_free = sem("dense_adj_free")
        x_diag = sem("dense_diag_made")
        x_tb = sem("dense_t_spread")
        x_tbc = sem("dense_t_copied")
        x_sc = sem("dense_scores_made")
        x_exp = sem("dense_exp_made")
        x_pr = sem("dense_weights_ready")
        x_stg = sem("dense_block_staged")
        x_tr = sem("dense_transposed")
        x_trc = sem("dense_transposed_copied")
        x_acc = sem("dense_summed")
        x_en = sem("dense_en_made")
        x_ex = sem("dense_ex_made")
        x_out = sem("dense_out_made")
        x_stored = sem("dense_out_stored")

        block = ctx.enter_context(nc.Block())

        def landed_by(quad):
            return sum(16 * slots_of(k, j) for k in range(quad + 1) if kind_of(k)[0] == kind_of(quad)[0]
                       for j in range(4))

        def landed_in_layer(quad):
            return landed_by(max(k for k in range(QUADS) if kind_of(k)[0] == kind_of(quad)[0]))

        TABLE_DMAS = 16 * (QUADS + 1)

        @block.sync
        def _(sp):
            sp.dma_start(REC[:, :, 0:F], x.rearrange("(t p) f -> p t f", p=P)).then_inc(x_loaded, 16)
            for l in range(4):
                sp.dma_start(WA[:, l, 0:F], Ws[l]).then_inc(w_loaded, 16)
            sp.wait_ge(av_set, 1)
            for l in (0, 1, 3):
                sp.dma_start(AV[:, l, 4:5], As[l][0:F, :]).then_inc(w_loaded, 16)
                sp.dma_start(AV[:, l, 0:1], As[l][F:2 * F, :]).then_inc(w_loaded, 16)
            D = F // 4
            for h in range(4):
                sp.dma_start(AV[h * D:(h + 1) * D, 2, 4 + h:5 + h],
                             As[2][0, h, 0:D].rearrange("(d a) -> d a", a=1)).then_inc(w_loaded, 16)
                sp.dma_start(AV[h * D:(h + 1) * D, 2, h:h + 1],
                             As[2][0, h, D:2 * D].rearrange("(d a) -> d a", a=1)).then_inc(w_loaded, 16)

            def load_adj(t, h):
                sp.dma_start(AREA[:, h % 4, :], adj[bass.ds(t * P, P), (h % 2) * HALF:(h % 2 + 1) * HALF]
                             ).then_inc(adj_loaded[h % 4], 16)

            for h in range(4):
                load_adj(h // 2, h)
            with sp.Fori(1, T // 2) as i:
                for h in range(4):
                    sp.wait_ge(mask_made, 4 * i + h - 3)
                    load_adj(2 * i + h // 2, h)

            def table_rows(l, t, n):
                return tab_d[bass.ds(l % 2 * NT + t * P, n * P), :].rearrange("(t p) w -> p t w", p=P)

            def store_mean(l):
                sp.wait_ge(meanrow_made, l + 1)
                sp.dma_start(tab_d[l % 2 * NT + N:l % 2 * NT + NT, :], MEANR[:]).then_inc(table_stored, 16)

            sp.wait_ge(rank_ready, 1)
            sp.dma_start(table_rows(0, 0, T), TBL[:]).then_inc(table_stored, 16)
            sp.dma_start(table_rows(1, 0, T), TBL[:]).then_inc(table_stored, 16)
            store_mean(0)
            sp.dma_start(tab_d[NT + N:2 * NT, :], MEANR[:]).then_inc(table_stored, 16)
            sp.wait_ge(flag_ready, 1)
            overflow = sp.value_load(FLAGI[0:1, 0:1])
            with sp.If(overflow == 0):
                sp.wait_ge(rec_scattered, 16 * T)
                rec_v = rec_d.rearrange("(t p) w -> p t w", p=P)
                sp.dma_start(REC[:, 0:SMALL_TILES, :], rec_v[:, 0:SMALL_TILES, :]).then_inc(rec_loaded, 16)
                sp.wait_ge(rec_loaded, 16)
                sp.dma_start(REC[:, SMALL_TILES:T, :], rec_v[:, SMALL_TILES:T, :]).then_inc(rec_loaded, 16)
                for l in range(1, 4):
                    with sp.Fori(0, QUADS) as q:
                        sp.wait_ge(tb_made, T * l + 4 * q + 4)
                        sp.dma_start(table_rows(l, 4 * q, 4), TBL[:, bass.ds(4 * q, 4), :]
                                     ).then_inc(table_stored, 16)
                    store_mean(l)
                sp.wait_ge(out_stored, 16 * T)
            with sp.Else():
                for inst in range(len(INST)):
                    with sp.Fori(0, T) as t:
                        sp.wait_ge(x_adj_free, inst * T + t + 1)
                        sp.dma_start(X_ADJ, adj[bass.ds(t * P, P), :]).then_inc(x_adj, 16)
                sp.wait_ge(x_out, 1)
                sp.dma_start(out.rearrange("(t p) f -> p t f", p=P), REC[:, :, 0:F]).then_inc(x_stored, 16)
                sp.wait_ge(x_stored, 16)
                sp.wait_ge(table_stored, 64)

        @block.gpsimd
        def _(pool):
            g = nc.gpsimd
            bound = pool.to_reg(2 * NT - 1)
            row_bound = pool.to_reg(N - 1)
            g.memset(IDN[:], 0.0).then_inc(iotas, 1)
            g.memset(ONE[:], 1.0).then_inc(iotas, 1)
            pool.wait_ge(iotas, 2)
            g.affine_select(out=IDN[:], in_=IDN[:], compare_op=ALU.not_equal, fill=1.0, base=0,
                            pattern=[[-1, P]], channel_multiplier=1).then_inc(iotas, 1)
            g.iota(pair_code, pattern=[[2, N // 2]], base=ODD0, channel_multiplier=0).then_inc(iotas, 1)
            g.affine_select(out=LOWERF, in_=ONE[:], compare_op=ALU.is_gt, fill=0.0, base=1,
                            pattern=[[-1, P]], channel_multiplier=1).then_inc(lower_made, 1)
            g.iota(RANKU[:], pattern=[[P, T]], base=0, channel_multiplier=1).then_inc(iotas, 1)

            def decode(i):
                pool.wait_ge(codes_ready, i + 1)
                pool.nop(nofuse=True)
                g.tensor_scalar(D_R, CQ, 0.5, ROUND, ALU.mult, ALU.add)
                g.tensor_scalar(D_B, CQ, 32768.0, None, ALU.is_ge)
                pool.drain()
                g.tensor_scalar(D_R, D_R, -ROUND, 2.0, ALU.add, ALU.mult)
                pool.drain()
                g.tensor_tensor(D_T, CQ, D_R, ALU.subtract)
                pool.drain()
                g.tensor_tensor(D_ODD, D_T, D_T, ALU.mult)
                pool.drain()
                g.tensor_scalar(D_W, D_ODD, 1 / 256 - 1 / 257, 1 - 1 / 256, ALU.mult, ALU.add)
                pool.drain()
                g.tensor_tensor(D_W, D_W, D_B, ALU.mult)
                pool.drain()
                g.tensor_scalar(D_W, D_W, -1.0, 1.0, ALU.mult, ALU.add)
                pool.drain()
                g.tensor_tensor(D_Q, CQ, D_W, ALU.mult).then_inc(codes_taken, 1)
                pool.drain()
                g.tensor_scalar(D_Q, D_Q, 1.0, ROUND, ALU.mult, ALU.add)
                pool.drain()
                g.tensor_scalar(D_R, D_Q, -ROUND, float(-(ODD0 - 1)), ALU.add, ALU.add)
                g.tensor_scalar(D_T, D_Q, -ROUND, float(-(ODD0 - 2)), ALU.add, ALU.add)
                pool.drain()
                pool.wait_ge(lists_free, i + 1)
                pool.nop(nofuse=True)
                g.tensor_tensor(L32[:, :, 0:SLOTS], D_R, D_ODD, ALU.mult)
                g.tensor_tensor(L32[:, :, SLOTS:], D_T, D_B, ALU.mult).then_inc(decoded, 1)

            with pool.Fori(0, QUADS) as i:
                decode(i)

            def gather_layer(l, last):
                pool.wait_ge(table_stored, TABLE_DMAS * l + 64)
                pool.nop(nofuse=True)
                for q in range(QUADS):
                    if q == BIG_QUAD:
                        pool.wait_ge(lists_ready, 2)
                    if FIRST_RING < q < FIRST_LAST:
                        before = BIG_QUAD - 1 if q == FIRST_RING + 1 else q - 2
                        pool.wait_ge(g_free, QUADS * l + before + 1)
                        pool.nop(nofuse=True)
                    kind, buffer = kind_of(q)
                    for j in range(4):
                        for s in range(slots_of(q, j)):
                            t = 4 * q + j
                            pool.indirect_dma_start(
                                buffer[:, j, s, :], None, tab_d,
                                bass.IndirectOffsetOnAxis(ap=NLU[:, t, s:s + 1], axis=0),
                                bounds_check=bound, oob_is_err=False,
                            ).then_inc(gathered[kind], 16)
                    if last and q >= 2:
                        scatter_quad(q - 2)
                if last:
                    scatter_quad(QUADS - 2)
                    scatter_quad(QUADS - 1)

            def scatter_quad(q):
                pool.wait_ge(x_final, q + 1)
                for j in range(4):
                    t = 4 * q + j
                    pool.indirect_dma_start(out, bass.IndirectOffsetOnAxis(ap=IDU[:, t:t + 1], axis=0),
                                            REC[:, t, 0:F], None, bounds_check=row_bound, oob_is_err=False,
                                            ).then_inc(out_stored, 16)

            pool.wait_ge(flag_ready, 1)
            overflow = pool.value_load(FLAGI[0:1, 0:1])
            with pool.If(overflow == 0):
                for t in range(T):
                    pool.indirect_dma_start(rec_d, bass.IndirectOffsetOnAxis(ap=RANKU[:, t:t + 1], axis=0),
                                            REC[:, t, :], None, bounds_check=row_bound, oob_is_err=False,
                                            ).then_inc(rec_scattered, 16)
                pool.wait_ge(lists_ready, 1)
                with pool.Fori(0, 3) as l:
                    gather_layer(l, False)
                gather_layer(3, True)

        @block.tensor
        def _(pe):
            pe.wait_ge(w_loaded, 16 * 18)
            pe.wait_ge(iotas, 3)
            for l in range(4):
                nc.tensor.transpose(psT[0][:, 0:P], WA[:, l, 0:F], IDN[:]).then_inc(wt_made, 1)
                pe.wait_ge(wt_copied, l + 1)
                nc.tensor.matmul(psW[0][:, 0:8], WT[:], AV[:, l, :], start=True, stop=True).then_inc(wa_made, 1)
                pe.wait_ge(wa_copied, l + 1)

            def project(l, no, j, kept):
                pe.wait_ge(hn_made, no + 1)
                nc.tensor.transpose(psT[j % 2][:, 0:P], HN[:, j, :], IDN[:]).then_inc(ht_psum, 1)
                pe.wait_ge(ht_made, no + 1)
                if kept is not None:
                    pe.wait_ge(*kept)
                nc.tensor.matmul(psW[j][:, 0:TW], HT[:, j % 2, :], WA[:, l, :], start=True, stop=True
                                 ).then_inc(wh_made, 1)

            def project_quad(l, q):
                no = T * l + 4 * q
                for j in range(5):
                    if j < 4:
                        pe.wait_ge(hn_made, no + j + 1)
                        if j >= 2:
                            pe.wait_ge(ht_made, no + j - 1)
                        nc.tensor.transpose(psT[j % 2][:, 0:P], HN[:, j, :], IDN[:]).then_inc(ht_psum, 1)
                    if j >= 1:
                        pe.wait_ge(ht_made, no + j)
                        pe.wait_ge(tb_made, no)
                        nc.tensor.matmul(psW[j - 1][:, 0:TW], HT[:, (j - 1) % 2, :], WA[:, l, :],
                                         start=True, stop=True).then_inc(wh_made, 1)

            def average_quad(l, q):
                for j in range(4):
                    pe.wait_ge(tb_made, T * l + 4 * q + j + 1)
                    nc.tensor.matmul(psM[l % 2][:, 0:F], ONEN[:], TBL[:, 4 * q + j, 0:F],
                                     start=type(q) is int and q == 0 and j == 0,
                                     stop=type(q) is int and q == QUADS - 1 and j == 3,
                                     skip_group_check=True).then_inc(mean_made, 1)

            pe.wait_ge(consts, 1)
            for j in range(4):
                project(0, j, j, None)
            with pe.Fori(1, QUADS) as q:
                for j in range(4):
                    project(0, 4 * q + j, j, (raw_kept, 4 * q + j - 3))

            pe.wait_ge(raw_kept, T)
            pe.wait_ge(onehot_made, 1)
            flat = OHB.rearrange("p c t -> p (c t)")
            n = NC * T
            for i, c in enumerate(range(0, n, 512)):
                w = min(512, n - c)
                nc.tensor.matmul((psX[0], psX[1], psW[1])[i][:, 0:w], ONEB, flat[:, c:c + w], start=True, stop=True
                                 ).then_inc(prefix_made, 1)
            for i, c in enumerate(range(0, n, 512)):
                w = min(512, n - c)
                nc.tensor.matmul((psT[0], psT[1], psW[0])[i][:, 0:w], LOWER, flat[:, c:c + w], start=True, stop=True
                                 ).then_inc(prefix_made, 1)
            pe.wait_ge(miss_made, 1)
            nc.tensor.matmul(psM[1][:, 0:1], ONE[:], FLAG[:, 0:1], start=True, stop=True).then_inc(flag_summed, 1)
            average_quad(0, 0)
            with pe.Fori(1, QUADS - 1) as q:
                average_quad(0, q)
            average_quad(0, QUADS - 1)
            pe.wait_ge(flag_ready, 1)
            overflow = pe.value_load(FLAGI[0:1, 0:1])
            with pe.If(overflow == 0):
                for l in range(1, 4):
                    project_quad(l, 0)
                    average_quad(l, 0)
                    with pe.Fori(1, QUADS - 1) as q:
                        project_quad(l, q)
                        average_quad(l, q)
                    project_quad(l, QUADS - 1)
                    average_quad(l, QUADS - 1)
            with pe.Else():
                pe.nop(nofuse=True).then_inc(x_tb, 1)
                pe.nop(nofuse=True).then_inc(x_tr, 1)
                for inst, (l, h) in enumerate(INST):
                    D = F // HEADS[l]
                    with pe.Fori(0, T // 2) as i:
                        for b in range(2):
                            n = inst * T + 2 * i + b
                            pe.wait_ge(x_diag, n + 1)
                            nc.tensor.matmul(psX[b][:, 0:P], ONE[:], X_DIAG[:, b, :], start=True, stop=True
                                             ).then_inc(x_tb, 1)
                            pe.wait_ge(x_tbc, n + 1)
                    with pe.Fori(0, T) as t:
                        no = inst * T + t
                        pe.wait_ge(x_pr, no + 1)
                        nc.tensor.matmul(psM[1][:, 0:D], ZERO[:], ZERO[:, 0:D], start=True, stop=False,
                                         skip_group_check=True)
                        with pe.Fori(0, T // 8) as g:
                            for b in range(2):
                                pe.wait_ge(x_stg, no * (T // 4) + 2 * g + b + 1)
                                for c in range(4):
                                    tr = nc.tensor.transpose(psX[b][:, c * P:(c + 1) * P],
                                                             X_ST[:, b, c * P:(c + 1) * P], IDN[:])
                                tr.then_inc(x_tr, 1)
                                pe.wait_ge(x_trc, no * (T // 4) + 2 * g + b + 1)
                                for c in range(4):
                                    nc.tensor.matmul(psM[1][:, 0:D], X_PT[:, b, c * P:(c + 1) * P],
                                                     TBL[:, 8 * g + 4 * b + c, h * D:(h + 1) * D],
                                                     start=False, stop=False, skip_group_check=True)
                        nc.tensor.matmul(psM[1][:, 0:D], ZERO[:], ZERO[:, 0:D], start=False, stop=True,
                                         skip_group_check=True).then_inc(x_acc, 1)
                    if h == HEADS[l] - 1 and l < 3:
                        project_quad(l + 1, 0)
                        average_quad(l + 1, 0)
                        with pe.Fori(1, QUADS - 1) as q:
                            project_quad(l + 1, q)
                            average_quad(l + 1, q)
                        project_quad(l + 1, QUADS - 1)
                        average_quad(l + 1, QUADS - 1)

        @block.scalar
        def _(act):
            a = nc.scalar
            for l in range(4):
                act.wait_ge(wt_made, l + 1)
                a.activation(WT[:], psT[0][:, 0:P], ACT.Copy).then_inc(wt_copied, 1)
                act.wait_ge(wa_made, l + 1)
                a.activation(WA[:, l, F:TW], psW[0][:, 0:8], ACT.Copy).then_inc(wa_copied, 1)

            def centre(rows, moments, j):
                act.wait_ge(moments_made, moments)
                a.activation(HN[:, j, :], rows, ACT.Identity, bias=NM[:, j:j + 1]).then_inc(hn_made, 1)

            def rectify(no, j):
                act.wait_ge(ht_psum, no + 1)
                a.activation(HT[:, j % 2, :], psT[j % 2][:, 0:P], ACT.Relu).then_inc(ht_made, 1)

            def keep_raw(t, j):
                act.wait_ge(wh_made, t + 1)
                a.activation(TBL[:, t, :], psW[j][:, 0:TW], ACT.Copy).then_inc(raw_kept, 1)

            def centre_quad(l, q, first=0, last=4):
                for j in range(first, last):
                    centre(REC[:, 4 * q + j, 0:F], T + QUADS * l + q + 1, j)

            def rectify_quad(l, q, first=0, last=4):
                for j in range(first, last):
                    no = T * (l + 1) + 4 * q + j
                    if j >= 2:
                        act.wait_ge(wh_made, no - 1)
                    rectify(no, j)

            def keep_quad(l, q):
                act.wait_ge(rstd_made, QUADS + QUADS * l + q + 1)
                for j in range(4):
                    t = 4 * q + j
                    act.wait_ge(wh_made, T * (l + 1) + t + 1)
                    a.activation(TBL[:, t, :], psW[j][:, 0:TW], ACT.Copy, scale=RSTD[:, bass.ds(t, 1)]
                                 ).then_inc(tb_made, 1)

            act.wait_ge(consts, 1)

            def make_mask(i, h):
                act.wait_ge(adj_loaded[h % 4], 32 * i + 16 * (h // 4) + 16)
                if not (type(i) is int and i == 0 and h < 2):
                    act.wait_ge(mask_read, 8 * i + h - 1)
                a.activation(mask[:, h % 2, :], AREA[:, h % 4, :], ACT.Sigmoid, bias=C100[:], scale=200.0,
                             accum_out=DEGH[:, bass.ds(8 * i + h, 1)]).then_inc(mask_made, 1)

            def scale(t, rstds):
                act.drain()
                act.wait_ge(rstd_made, rstds)
                a.activation(TBL[:, t, :], TBL[:, t, :], ACT.Copy, scale=RSTD[:, bass.ds(t, 1)]).then_inc(tb_made, 1)

            def extract_quad(i):
                first = type(i) is int and i == 0
                for j in range(4):
                    t = 4 * i + j
                    make_mask(i, 2 * j)
                    if not (first and j < 2):
                        keep_raw(t - 2, (j - 2) % 4)
                    if not (first and j < 1):
                        centre(REC[:, t - 1, 0:F], t, (j - 1) % 4)
                    make_mask(i, 2 * j + 1)
                    if not (first and j < 1):
                        rectify(t - 1, (j - 1) % 4)
                    if type(i) is not int:
                        scale(t - 8, i - 1)

            extract_quad(0)
            extract_quad(1)
            with act.Fori(2, QUADS) as i:
                extract_quad(i)
            keep_raw(T - 2, 2)
            centre(REC[:, T - 1, 0:F], T, 3)
            rectify(T - 1, 3)
            keep_raw(T - 1, 3)
            for t in range(T - 8, T):
                scale(t, t // 4 + 1)

            def exp_scores(l, q, k):
                n = 4 * k * HEADS[l]
                act.wait_ge(sc_made, QUADS * l + q + 1)
                a.activation(PRB[:, 0:n], SCO[:, 0:n], ACT.Exp).then_inc(exp_made, 1)

            def exp_negative(l, q):
                act.wait_ge(h_made, QUADS * l + q + 1)
                a.activation(NEG, HH, ACT.Relu, scale=-1.0)
                act.drain()
                a.activation(EX[:], NEG, ACT.Exp, scale=-1.0).then_inc(ex_made, 1)

            act.wait_ge(flag_ready, 1)
            overflow = act.value_load(FLAGI[0:1, 0:1])
            with act.If(overflow == 0):
                for l in range(4):
                    def quad(q):
                        exp_negative(l, q)
                        if l < 3:
                            centre_quad(l, q, 0, 2)
                            rectify_quad(l, q, 0, 1)
                            centre_quad(l, q, 2, 3)
                            rectify_quad(l, q, 1, 2)
                            centre_quad(l, q, 3, 4)
                        if type(q) is not int:
                            exp_scores(l, q + 1, QMAX)
                        elif q < QUADS - 1:
                            exp_scores(l, q + 1, score_slots(q + 1))
                        if l < 3:
                            rectify_quad(l, q, 2, 4)
                            keep_quad(l, q)

                    exp_scores(l, 0, score_slots(0))
                    for q in range(FIRST_RING):
                        quad(q)
                    with act.Fori(FIRST_RING, AFTER_RUNS) as q:
                        quad(q)
                    for q in range(AFTER_RUNS, QUADS):
                        quad(q)
            with act.Else():
                for inst, (l, h) in enumerate(INST):
                    D = F // HEADS[l]
                    with act.Fori(0, T // 2) as i:
                        for b in range(2):
                            act.wait_ge(x_tb, inst * T + 2 * i + b + 2)
                            nc.scalar.activation(X_T[:, bass.ds(i * (2 * P) + b * P, P)], psX[b][:, 0:P], ACT.Copy
                                                 ).then_inc(x_tbc, 1)
                    with act.Fori(0, T) as t:
                        no = inst * T + t
                        act.wait_ge(x_sc, no + 1)
                        nc.scalar.activation(X_E, X_E, ACT.Exp, bias=X_M[:, 1:2], accum_out=X_M[:, 2:3]
                                             ).then_inc(x_exp, 1)
                        with act.Fori(0, T // 8) as g:
                            for b in range(2):
                                act.wait_ge(x_tr, no * (T // 4) + 2 * g + b + 2)
                                nc.scalar.activation(X_PT[:, b, :], psX[b][:], ACT.Copy).then_inc(x_trc, 1)
                        act.wait_ge(x_en, no + 1)
                        nc.scalar.activation(X_E1[:, 0:D], X_H[:, 0:D], ACT.Exp).then_inc(x_ex, 1)
                    if h == HEADS[l] - 1 and l < 3:
                        with act.Fori(0, QUADS) as q:
                            centre_quad(l, q)
                            rectify_quad(l, q)
                            keep_quad(l, q)

        def moments(dve, v, q):
            for j in range(4):
                v.bn_stats(ST[:, j, :], REC[:, 4 * q + j, 0:F])
            dve.drain()
            for j in range(4):
                v.bn_aggr(MV[:, j, :], ST[:, j, :])
            dve.drain()
            v.tensor_scalar(NM[:], MV[:, :, 0], -1.0, None, ALU.mult).then_inc(moments_made, 1)
            v.tensor_scalar(VAR[:, bass.ds(4 * q, 4)], MV[:, :, 1], EPS, None, ALU.add)

        def seed_bits(v, t, n, step):
            at = bass.ds(t, n)
            if step == 0:
                v.tensor_scalar(SEED[:, 0:n], VAR[:, at].bitcast(I32), 1, None, ALU.arith_shift_right)
            else:
                v.tensor_scalar(RSTD[:, at].bitcast(I32), SEED[:, 0:n], -1.0, float(0x5F3759DF),
                                ALU.mult, ALU.add)

        def newton(v, t, n, step):
            at = bass.ds(t, n)
            y, u = RSTD[:, at], NEWT[:, 0:n]
            if step == 0:
                return v.tensor_tensor(u, y, y, ALU.mult)
            if step == 1:
                return v.scalar_tensor_tensor(u, u, -0.5, VAR[:, at], ALU.mult, ALU.mult)
            return v.scalar_tensor_tensor(y, u, 1.5, y, ALU.add, ALU.mult)

        def deviations(dve, v, t, n):
            dve.drain()
            for step in range(2):
                seed_bits(v, t, n, step)
                dve.drain()
            for step in range(9):
                last = newton(v, t, n, step % 3)
                if step < 8:
                    dve.drain()
            last.then_inc(rstd_made, 1)

        def fast(dve, v):
            v.memset(area[:, 0:RING_BASE + 8 * QMAX * TW].bitcast(F32), 0.0)

            def read_lists(t, n):
                at = bass.ds(t, n)
                NL = REC[:, at, R_NL:R_NL + SLOTS]
                pads = PR[:, 0:n * SLOTS].rearrange("p (t s) -> p t s", s=SLOTS)
                v.tensor_scalar(VB[:, at, :], NL, 0.0, -BIG, ALU.is_equal, ALU.mult)
                v.tensor_scalar(pads, NL, 0.0, 8.0 * N, ALU.is_equal, ALU.mult)
                v.tensor_copy(IDU[:, at], REC[:, at, R_ID])
                dve.drain()
                v.memset(VB[:, at, 0:1], 0.0)
                v.tensor_scalar(pads[:, :, 0:1], pads[:, :, 0:1], (N + 1) / (8.0 * N), None, ALU.mult)
                dve.drain()
                v.scalar_tensor_tensor(NLU[:, at, :], NL, -1.0, pads, ALU.add, ALU.add)
                dve.drain()

            dve.wait_ge(rec_loaded, 16)
            read_lists(0, SMALL_TILES)
            v.memset(MX[:, 0:1], 0.0).then_inc(lists_ready, 1)
            dve.wait_ge(rec_loaded, 32)
            read_lists(SMALL_TILES, T - SMALL_TILES)
            v.memset(MX[:, 0:1], 0.0).then_inc(lists_ready, 1)

            for l in range(4):
                if l > 0:
                    mean_row(dve, v, l)
                scores(dve, v, l, 0, 0)

                def quad(q, sample, slots, run):
                    attend(dve, v, l, q, sample, slots)
                    update(dve, v, l, q)
                    if sample < QUADS - 1:
                        scores(dve, v, l, q + 1, sample + 1, run)

                for q in range(FIRST_RING):
                    quad(q, q, slots_of(q, 0), None)
                for first, slots in PAIR_RUNS:
                    with dve.Fori(first, first + 4, 2) as q:
                        for b in range(2):
                            quad(q + b, first + b, slots, first + b + 1)
                for q in range(AFTER_RUNS, QUADS):
                    quad(q, q, slots_of(q, 0), None)
                if l < 3:
                    deviations(dve, v, T - 4, 4)

        def mean_row(dve, v, l):
            dve.wait_ge(mean_made, T * (l + 1))
            v.tensor_copy(MEANR[:, 0:F], psM[l % 2][0:1, 0:F])
            v.memset(MEANR[:, T_AUX:T_AUX + 1], 0.0).then_inc(meanrow_made, 1)

        def scores(dve, v, l, q, sample, run=None):
            H = HEADS[l]
            k = score_slots(sample)
            n = 4 * k * H
            kind, g = kind_of(sample)
            tiles = bass.ds(4 * q, 4)
            sco = SCO[:, 0:n].rearrange("p (j s h) -> p j s h", j=4, h=H)
            per_slot = lambda ap: ap.unsqueeze(2).to_broadcast([P, 4, k, H])
            heads = lambda ap: ap[:, 0:4 * H].rearrange("p (j h) -> p j h", j=4)
            aux1 = AUX1[:, 0:4 * k].rearrange("p (j s) -> p j s", j=4)
            at = None if sample == 0 or l == 3 else 4 * q - 4
            src = REC[:, tiles, R_S:R_S + H] if l == 0 else TBL[:, tiles, T_S:T_S + H]

            if l > 0 and sample == 0:
                dve.wait_ge(tb_made, T * (l + 1))
            if run is None:
                dve.wait_ge(gathered[kind], l * landed_in_layer(q) + landed_by(q))
            else:
                step = (landed_by(run + 2) - landed_by(run)) // 2
                dve.wait_ge(gathered[kind], q * step + (l * landed_in_layer(run) + landed_by(run) - step * run))
            v.tensor_tensor(sco, g[:, :, 0:k, T_T:T_T + H], per_slot(src), ALU.add)
            if l == 1:
                v.tensor_scalar(aux1, g[:, :, 0:k, T_AUX], 0.0, 1.0, ALU.not_equal, ALU.subtract)
            if at is not None:
                seed_bits(v, at, 4, 0)
            dve.drain()
            v.scalar_tensor_tensor(SCO[:, 0:n], SCO[:, 0:n], ALPHA, SCO[:, 0:n], ALU.mult, ALU.max)
            if l == 1:
                v.scalar_tensor_tensor(aux1, aux1, BIG, VB[:, tiles, 0:k], ALU.mult, ALU.add)
            if at is not None:
                seed_bits(v, at, 4, 1)
            dve.drain()
            if l == 1:
                v.tensor_tensor(SCO[:, 0:n], SCO[:, 0:n], AUX1[:, 0:n], ALU.add)
                v.tensor_scalar(AUX2[:, 0:n], AUX1[:, 0:n], 0.0, None, ALU.is_equal)
            else:
                v.tensor_tensor(sco, sco, VB[:, tiles, 0:k].unsqueeze(3).to_broadcast([P, 4, k, H]), ALU.add)
            if at is not None:
                newton(v, at, 4, 0)
            dve.drain()
            v.tensor_reduce(heads(MX), sco.rearrange("p j s h -> p j h s"), AX.X, ALU.max)
            if l == 1:
                v.tensor_reduce(LCNT, AUX2[:, 0:n].rearrange("p (j s) -> p j s", j=4), AX.X, ALU.add)
            if at is not None:
                newton(v, at, 4, 1)
            dve.drain()
            v.tensor_tensor(sco, sco, per_slot(heads(MX)), ALU.subtract).then_inc(sc_made, 1)
            if at is not None:
                last = newton(v, at, 4, 2)
                for step in range(3, 9):
                    dve.drain()
                    last = newton(v, at, 4, step % 3)
                last.then_inc(rstd_made, 1)

        def attend(dve, v, l, q, sample, k):
            H = HEADS[l]
            kk = score_slots(sample)
            g = kind_of(sample)[1]
            n = 4 * kk * H
            tiles = bass.ds(4 * q, 4)
            prb = PRB[:, 0:n].rearrange("p (j s h) -> p j s h", j=4, h=H)
            per_slot = lambda ap: ap.unsqueeze(2).to_broadcast([P, 4, kk, H])
            heads = lambda ap: ap[:, 0:4 * H].rearrange("p (j h) -> p j h", j=4)
            pr = PR[:, 0:4 * k * F].rearrange("p (j s f) -> p j s f", j=4, f=F)
            dve.wait_ge(exp_made, QUADS * l + q + 1)
            v.tensor_reduce(heads(Z), prb.rearrange("p j s h -> p j h s"), AX.X, ALU.add)
            dve.drain()
            v.reciprocal(RZ[:, 0:4 * H], Z[:, 0:4 * H])
            dve.drain()
            v.tensor_tensor(prb, prb, per_slot(heads(RZ)), ALU.mult)
            if l == 1:
                v.scalar_tensor_tensor(COUNT, RZ[:, 0:4], THR, LCNT, ALU.is_gt, ALU.mult)
            dve.drain()
            if l == 1:
                v.scalar_tensor_tensor(AUX1[:, 0:n], PRB[:, 0:n], THR, PRB[:, 0:n], ALU.is_ge, ALU.mult)
                dve.drain()
                v.tensor_tensor(prb[:, :, :, 0], AUX1[:, 0:n].rearrange("p (j s) -> p j s", j=4),
                                COUNT.unsqueeze(2).to_broadcast([P, 4, kk]), ALU.mult)
                dve.drain()
            if H == 1:
                used = v.tensor_tensor(pr, g[:, :, 0:k, 0:F], prb[:, :, 0:k, :].to_broadcast([P, 4, k, F]), ALU.mult)
            else:
                for j in range(4):
                    used = v.tensor_tensor(pr[:, j].rearrange("p s (h d) -> p s h d", h=H),
                                    g[:, j, 0:k, 0:F].rearrange("p s (h d) -> p s h d", h=H),
                                    prb[:, j, 0:k, :].unsqueeze(3).to_broadcast([P, k, H, F // H]), ALU.mult)
            if l == 0:
                used = v.scalar_tensor_tensor(NLU[:, tiles, 0:k], VB[:, tiles, 0:k], -8.0 * N / BIG,
                                              g[:, :, 0:k, T_AUX], ALU.mult, ALU.add)
            elif l < 3:
                used = v.tensor_scalar(NLU[:, tiles, :], NLU[:, tiles, :], float(NT if l == 2 else -NT), None,
                                       ALU.add)
            used.then_inc(g_free, 1)
            dve.drain()
            summed = v.tensor_reduce(HH, pr.rearrange("p j s f -> p j f s"), AX.X, ALU.add)
            if l == 1:
                dve.drain()
                summed = v.tensor_tensor(HH, HH, TBL[:, tiles, 0:F], ALU.add)
            summed.then_inc(h_made, 1)

        def update(dve, v, l, q):
            rows = REC[:, bass.ds(4 * q, 4), 0:F]
            dve.drain()
            v.scalar_tensor_tensor(POS, HH, 0.0, rows, ALU.max, ALU.add)
            dve.drain()
            dve.wait_ge(ex_made, QUADS * l + q + 1)
            if l == 3:
                v.scalar_tensor_tensor(rows, EX[:], -1.0, POS, ALU.add, ALU.add).then_inc(x_final, 1)
            else:
                v.scalar_tensor_tensor(rows, EX[:], -1.0, POS, ALU.add, ALU.add)
                dve.drain()
                moments(dve, v, q)
                dve.drain()

        def dense(dve, v):
            for inst, (l, h) in enumerate(INST):
                D = F // HEADS[l]
                if h == 0:
                    dve.wait_ge(mean_made, T * (l + 1))
                    v.tensor_copy(MEAN[:], psM[l % 2][:, 0:F])
                v.tensor_copy(X_TC, TBL[:, :, T_T + h])
                if l == 1:
                    v.tensor_scalar(X_TG, TBL[:, :, T_AUX], 0.0, 1.0, ALU.not_equal, ALU.subtract)
                    dve.drain()
                    v.scalar_tensor_tensor(X_TC, X_TG, BIG, X_TC, ALU.mult, ALU.add)
                dve.drain()
                with dve.Fori(0, T // 2) as i:
                    for b in range(2):
                        dve.wait_ge(x_tb, inst * T + 2 * i + b + 1)
                        v.tensor_scalar(X_DIAG[:, b, :], IDN[:], X_TC[:, bass.ds(2 * i + b, 1)], None, ALU.mult
                                        ).then_inc(x_diag, 1)
                dve.wait_ge(x_tbc, (inst + 1) * T)
                with dve.Fori(0, T) as t:
                    no = inst * T + t
                    v.memset(X_M[:, 3:4], 0.0).then_inc(x_adj_free, 1)
                    dve.wait_ge(x_adj, 16 * no + 16)
                    v.tensor_scalar(X_BIAS, X_ADJ, 0.0, 1.0, ALU.is_gt, ALU.subtract)
                    v.tensor_scalar(X_E, X_T, TBL[:, t, T_S + h:T_S + h + 1], None, ALU.add)
                    dve.drain()
                    v.scalar_tensor_tensor(X_E, X_E, ALPHA, X_E, ALU.mult, ALU.max)
                    dve.drain()
                    v.scalar_tensor_tensor(X_E, X_BIAS, BIG, X_E, ALU.mult, ALU.add)
                    dve.drain()
                    v.tensor_reduce(X_M[:, 0:1], X_E, AX.X, ALU.max)
                    if l == 1:
                        v.tensor_scalar(X_BIAS, X_E, FLOOR, None, ALU.is_gt)
                        dve.drain()
                        v.tensor_reduce(X_M[:, 3:4], X_BIAS, AX.X, ALU.add)
                    dve.drain()
                    v.tensor_scalar(X_M[:, 1:2], X_M[:, 0:1], FLOOR, -1.0, ALU.max, ALU.mult).then_inc(x_sc, 1)
                    dve.wait_ge(x_exp, no + 1)
                    v.tensor_scalar(X_M[:, 4:5], X_M[:, 2:3], 1e-30, None, ALU.max)
                    v.tensor_scalar(X_M[:, 6:7], X_M[:, 2:3], 0.0, None, ALU.is_equal)
                    dve.drain()
                    v.reciprocal(X_M[:, 5:6], X_M[:, 4:5])
                    dve.drain()
                    if l == 1:
                        v.tensor_scalar(X_E, X_E, X_M[:, 5:6], None, ALU.mult)
                        dve.drain()
                        v.tensor_reduce(X_M[:, 7:8], X_E, AX.X, ALU.max)
                        v.scalar_tensor_tensor(X_E, X_E, THR, X_E, ALU.is_ge, ALU.mult)
                        dve.drain()
                        v.scalar_tensor_tensor(X_M[:, 5:6], X_M[:, 7:8], THR, X_M[:, 3:4], ALU.is_gt, ALU.mult)
                        dve.drain()
                        v.tensor_copy(X_H[:, 0:D], TBL[:, t, 0:D]).then_inc(x_pr, 1)
                    else:
                        v.tensor_scalar(X_H[:, 0:D], MEAN[:, h * D:(h + 1) * D], X_M[:, 6:7], None, ALU.mult
                                        ).then_inc(x_pr, 1)
                    dve.drain()
                    with dve.Fori(0, T // 8) as g:
                        for b in range(2):
                            dve.wait_ge(x_tr, no * (T // 4) + 2 * g + b + 1)
                            v.tensor_copy(X_ST[:, b, :], X_E[:, bass.ds(g * (8 * P) + b * (4 * P), 4 * P)]
                                          ).then_inc(x_stg, 1)
                    dve.wait_ge(x_acc, no + 1)
                    v.scalar_tensor_tensor(X_H[:, 0:D], psM[1][:, 0:D], X_M[:, 5:6], X_H[:, 0:D], ALU.mult, ALU.add)
                    dve.drain()
                    x_rows = REC[:, t, h * D:(h + 1) * D]
                    v.scalar_tensor_tensor(x_rows, X_H[:, 0:D], 0.0, x_rows, ALU.max, ALU.add)
                    v.tensor_scalar(X_H[:, 0:D], X_H[:, 0:D], 0.0, None, ALU.min).then_inc(x_en, 1)
                    dve.drain()
                    dve.wait_ge(x_ex, no + 1)
                    v.scalar_tensor_tensor(x_rows, X_E1[:, 0:D], -1.0, x_rows, ALU.add, ALU.add)
                    dve.drain()
                if h == HEADS[l] - 1 and l < 3:
                    with dve.Fori(0, QUADS) as q:
                        dve.wait_ge(hn_made, T * (l + 1) + 4 * q)
                        moments(dve, v, q)
                        deviations(dve, v, 4 * q, 4)
            v.memset(X_M[:, 0:1], 0.0).then_inc(x_out, 1)

        @block.vector
        def _(dve):
            v = nc.vector
            v.memset(AV[:], 0.0)
            dve.drain()
            v.memset(AV[:, 1, 1:2], 1.0).then_inc(av_set, 1)
            v.memset(ONEN[:], 1.0 / N)
            v.memset(ZERO[:], 0.0)
            v.memset(MEANR[:], 0.0)
            v.memset(C100[:], -100.0).then_inc(consts, 1)
            dve.wait_ge(x_loaded, 16)
            dve.wait_ge(iotas, 5)
            v.tensor_copy(REC[:, :, R_ID], RANKU[:])
            v.memset(REC[:, :, R_ID + 1:RW], 0.0).then_inc(lists_free, 1)

            def codes_of(i, j, half):
                dve.wait_ge(mask_made, 8 * i + 2 * j + half + 1)
                v.tensor_tensor(code[:, half, :], mask[:, half, :].bitcast(U16),
                                pair_code[:, half * HP:(half + 1) * HP], ALU.mult).then_inc(mask_read, 1)

            def candidates(j, half):
                for s in range(SEGS):
                    at = (half * SEGS + s) * 8
                    v.max(CND[:, j % 2, at:at + 8], code[:, half, s * SEG:(s + 1) * SEG])

            def hand_codes(j, first):
                op = v.tensor_copy(CQ[:, j, :], TOP[:, j, :])
                if j == 3:
                    op.then_inc(codes_ready, 1)

            def lists_largest(n):
                dve.wait_ge(decoded, n)
                dve.nop(nofuse=True)
                for j in range(4):
                    v.max(S16[:, j, 0:8], L32[:, j, :])

            def lists_replace():
                for j in range(4):
                    op = v.match_replace(S32[:, j, :], S16[:, j, 0:8], L32[:, j, :], 0.0)
                op.then_inc(lists_free, 1)

            def lists_next():
                for j in range(4):
                    v.max(S16[:, j, 8:16], S32[:, j, :])

            def extract_quad(i):
                first = type(i) is int

                def deviation_step(step):
                    if step < 2:
                        return seed_bits(v, 4 * i - 4, 4, step)
                    return newton(v, 4 * i - 4, 4, (step - 2) % 3)

                for j in range(4):
                    t = 4 * i + j
                    p1, p2 = (j - 1) % 4, (j - 2) % 4
                    codes_of(i, j, 0)
                    v.bn_stats(ST[:, j, :], REC[:, t, 0:F])
                    if not first and j > 0:
                        deviation_step(2 * j - 1)
                    dve.drain()
                    candidates(j, 0)
                    if not (first and j < 1):
                        v.max(TOP[:, p1, 0:8], CND[:, p1 % 2, :])
                    if not (first and j < 2):
                        v.max(TOP[:, p2, 8:16], CND2)
                    v.bn_aggr(MV[:, j, :], ST[:, j, :])
                    if not first and j == 3:
                        lists_replace()
                    codes_of(i, j, 1)
                    if not first:
                        deviation_step(2 * j)
                    dve.drain()
                    candidates(j, 1)
                    if not (first and j < 1):
                        v.match_replace(CND2, TOP[:, p1, 0:8], CND[:, p1 % 2, :], 0.0)
                    v.tensor_scalar(NM[:, j:j + 1], MV[:, j, 0:1], -1.0, None, ALU.mult).then_inc(moments_made, 1)
                    v.tensor_scalar(VAR[:, bass.ds(t, 1)], MV[:, j, 1:2], EPS, None, ALU.add)
                    if not first and j == 2:
                        dve.wait_ge(codes_taken, i)
                    if not (first and j < 2):
                        hand_codes(p2, first)
                    if not first and j == 2:
                        lists_largest(i)
                    if not first and j == 3:
                        lists_next()
                        for step in range(7, 11):
                            deviation = deviation_step(step)
                            dve.drain()
                        deviation.then_inc(rstd_made, 1)
                        v.tensor_copy(REC[:, bass.ds(4 * i - 4, 4), R_NL:R_NL + SLOTS], S16)

            extract_quad(0)
            with dve.Fori(1, QUADS) as i:
                extract_quad(i)
            dve.drain()
            v.max(TOP[:, 3, 0:8], CND[:, 1, :])
            v.max(TOP[:, 2, 8:16], CND2)
            dve.drain()
            v.match_replace(CND2, TOP[:, 3, 0:8], CND[:, 1, :], 0.0)
            hand_codes(2, False)
            dve.drain()
            v.max(TOP[:, 3, 8:16], CND2)
            dve.drain()
            hand_codes(3, False)
            deviations(dve, v, T - 4, 4)

            v.tensor_tensor(DEG[:], DEGH[:, 0:2 * T:2], DEGH[:, 1:2 * T:2], ALU.add)
            for k in range(NC):
                v.memset(CLS[:, k, :], float(SLOTS - k))
            v.memset(ONEB, 1.0)
            dve.wait_ge(lower_made, 1)
            v.tensor_copy(LOWER, LOWERF)
            dve.drain()
            v.tensor_scalar(DEG[:], DEG[:], ROUND, None, ALU.add)
            dve.drain()
            v.tensor_scalar(DEG[:], DEG[:], ROUND, None, ALU.subtract)
            dve.drain()
            v.tensor_scalar(DCAP, DEG[:], float(SLOTS), None, ALU.min)
            dve.drain()
            v.tensor_tensor(OHB, CLS, DCAP.unsqueeze(1).to_broadcast([P, NC, T]), ALU.is_equal
                            ).then_inc(onehot_made, 1)
            lists_largest(QUADS)
            dve.drain()
            lists_replace()
            dve.drain()
            lists_next()
            dve.drain()
            v.tensor_copy(REC[:, T - 4:T, R_NL:R_NL + SLOTS], S16)
            dve.drain()
            v.tensor_scalar(VALID, REC[:, :, R_NL:R_NL + SLOTS], 0.0, None, ALU.is_gt)

            def bank(i):
                return i * 512, min(512, NC * T - i * 512)

            tot = TOT.rearrange("p c t -> p (c t)")
            dve.wait_ge(prefix_made, 3)
            for i, src in enumerate((psX[0], psX[1], psW[1])):
                at, w = bank(i)
                v.tensor_copy(tot[:, at:at + w], src[:, 0:w])
            dve.drain()
            sums = SUMS.rearrange("p c t -> p (c t)")
            v.tensor_tensor_scan(sums, tot, tot, 0.0, ALU.add, ALU.max)
            v.tensor_reduce(CNT, VALID, AX.X, ALU.add)
            v.memset(FAULTS, 0.0)
            dve.drain()
            v.tensor_tensor(MIS, CNT, DEG[:], ALU.not_equal)
            slots_before = SLOTS
            for t in range(T):
                k = BY_DEGREE[t]
                if k < slots_before:
                    v.tensor_scalar(FAULTS[:, k:k + 1], SUMS[:, SLOTS - k - 1, T - 1:T], P * t + 0.5, None,
                                    ALU.is_gt)
                    slots_before = k
            dve.drain()
            v.tensor_reduce(FAULTS[:, 0:1], MIS, AX.X, ALU.add)
            dve.wait_ge(prefix_made, 6)
            for i, src in enumerate((psT[0], psT[1], psW[0])):
                at, w = bank(i)
                v.tensor_tensor(tot[:, at:at + w], sums[:, at:at + w], src[:, 0:w], ALU.subtract)
            dve.drain()
            v.tensor_reduce(FLAG[:, 0:1], FAULTS, AX.X, ALU.add)
            v.tensor_tensor(SUMS, TOT, OHB, ALU.mult)
            dve.drain()
            v.tensor_copy(FLAG[:, 1:2], FLAG[:, 0:1]).then_inc(miss_made, 1)
            v.tensor_reduce(RANKF[:], SUMS.rearrange("p c t -> p t c"), AX.X, ALU.add)
            dve.drain()
            v.tensor_scalar(CNT, RANKF[:], N - SHIFT - 0.5, -float(N), ALU.is_gt, ALU.mult)
            dve.drain()
            v.scalar_tensor_tensor(RANKF[:], RANKF[:], float(SHIFT), CNT, ALU.add, ALU.add)
            dve.drain()
            v.tensor_copy(RANKU[:], RANKF[:])
            dve.wait_ge(tb_made, T)
            v.tensor_scalar(TBL[:, :, T_AUX], RANKF[:], float(NT), None, ALU.add)
            v.tensor_copy(REC[:, :, R_S:R_S + 4], TBL[:, :, T_S:T_S + 4]).then_inc(rank_ready, 1)
            dve.wait_ge(flag_summed, 1)
            v.tensor_copy(FLAGI[:], psM[1][:, 0:1]).then_inc(flag_ready, 1)
            dve.wait_ge(mean_made, T)
            v.tensor_copy(MEANR[:, 0:F], psM[0][0:1, 0:F])
            v.memset(MEANR[:, T_AUX:T_AUX + 1], float(N + NT)).then_inc(meanrow_made, 1)
            dve.wait_ge(flag_ready, 1)
            overflow = dve.value_load(FLAGI[0:1, 0:1])
            with dve.If(overflow == 0):
                fast(dve, v)
            with dve.Else():
                dense(dve, v)


_INS = ["x", "adj", "L0_gnn_W", "L0_gnn_a", "L1_gnn_W", "L1_gnn_a", "L2_gnn_W", "L2_gnn_a",
        "L3_gnn_W", "L3_gnn_a"]
_OUTS = [((8192, 128), "float32")]


def kernel(**inputs):
    import numpy as _np
    import concourse.bacc as _bacc
    from concourse import mybir as _mybir
    from concourse.bass_utils import run_bass_kernel_spmd as _run

    nc = _bacc.Bacc("TRN2", target_bir_lowering=False, num_devices=1)
    arrays, args = {}, []
    for name in _INS:
        a = _np.ascontiguousarray(inputs[name])
        arrays[f"in_{name}_dram"] = a
        args.append(nc.dram_tensor(f"in_{name}_dram", a.shape, _mybir.dt.from_np(a.dtype), kind="ExternalInput").ap())
    for i, (shape, dtype) in enumerate(_OUTS):
        dt = _mybir.dt.from_np(_np.dtype(dtype))
        args.append(nc.dram_tensor(f"out_{i}_dram", shape, dt, kind="ExternalOutput").ap())
    gat_kernel(nc, *args)
    r = _run(nc, [arrays], core_ids=[0])
    return r.results[0]["out_0_dram"]
```
